# Optimizing a Trainium2 kernel written in Bass

```python
import numpy as np
import jax
import jax.numpy as jnp

def _softmax(x, axis=-1):
    return jax.nn.softmax(x, axis=axis)

def _gelu(x):
    return jax.nn.gelu(x, approximate=True)

def _silu(x):
    return jax.nn.silu(x)

def _sigmoid(x):
    return jax.nn.sigmoid(x)

def _layernorm(x, axis=-1, eps=1e-05):
    m = jnp.mean(x, axis=axis, keepdims=True)
    v = jnp.var(x, axis=axis, keepdims=True)
    return (x - m) / jnp.sqrt(v + eps)

def _scatter_add(tgt, idx, src, axis=0):
    return tgt.at[idx].add(src)

def _segment_sum(src, seg, n):
    return jax.ops.segment_sum(src, seg, n)
kernel_name = 'mk_adj_ffn_d1_adj_r2_f2d2fd'

def setup_inputs(seed: int=0):
    np.random.seed(seed)
    _w = jnp.asarray

    def _rec_inputs():
        import jax
        import jax.numpy as jnp
        _gk = jax.random.key(seed)
        x = -8.776e-05 + 1 * jax.random.normal(jax.random.fold_in(_gk, 1), (10000, 128), jnp.float32)
        _w = (1.0 + jnp.arange(10000, dtype=jnp.float32)) ** (-0.5)
        _w = _w / _w.mean()
        _pij = jnp.clip(0.0016 * _w[:, None] * _w[None, :], 0.0, 1.0)
        _a = jax.random.uniform(jax.random.fold_in(_gk, 2), (10000, 10000)) < _pij
        _a = jnp.logical_or(_a, jnp.eye(10000, dtype=bool))
        _af = _a.astype(jnp.float32)
        _af = _af * jax.random.uniform(jax.random.fold_in(_gk, 3), (10000, 10000), jnp.float32, 0.05, 1)
        adj = _af
        return (x, adj)
    x, adj = _rec_inputs()

    def _L0_gnn_setup():
        import jax, jax.numpy as jnp
        import numpy as np
        N_USER = 10000
        N_ITEM = 10000
        HID = 128
        key = jax.random.key(seed)
        k1, k2, k3, k4, k5, k6, k7 = jax.random.split(key, 7)
        scale = 1.0 / np.sqrt(HID)
        return {'user_feat': jax.random.normal(k1, (N_USER, HID), dtype=jnp.float32), 'item_feat': jax.random.normal(k2, (N_ITEM, HID), dtype=jnp.float32), 'adj': jax.random.uniform(k3, (N_USER, N_ITEM), dtype=jnp.float32), 'W_item': jax.random.uniform(k4, (HID, HID), dtype=jnp.float32, minval=-scale, maxval=scale), 'b_item': jax.random.uniform(k5, (HID,), dtype=jnp.float32, minval=-scale, maxval=scale), 'W_user': jax.random.uniform(k6, (HID, HID), dtype=jnp.float32, minval=-scale, maxval=scale), 'b_user': jax.random.uniform(k7, (HID,), dtype=jnp.float32, minval=-scale, maxval=scale)}
    _L0_gnn_all = _L0_gnn_setup()
    _L0_gnn_in = {k: v for k, v in _L0_gnn_all.items() if k in ('item_feat', 'W_item', 'b_item', 'W_user', 'b_user')}
    del _L0_gnn_all

    def _L0_ffn_setup():
        import jax, jax.numpy as jnp
        import numpy as np
        B, T, D, H, L = (16, 2048, 128, 128, 2)

        def _lstm(x, W_ih, W_hh, b_ih, b_hh):
            x_proj = jnp.einsum('btd,gd->btg', x, W_ih) + b_ih + b_hh
            h0 = jnp.zeros((x.shape[0], W_hh.shape[1]), x.dtype)
            c0 = jnp.zeros_like(h0)

            def step(carry, xp):
                h, c = carry
                gates = xp + h @ W_hh.T
                i, f, g, o = jnp.split(gates, 4, axis=-1)
                c = jax.nn.sigmoid(f) * c + jax.nn.sigmoid(i) * jnp.tanh(g)
                h = jax.nn.sigmoid(o) * jnp.tanh(c)
                return ((h, c), h)
            _, hs = jax.lax.scan(step, (h0, c0), jnp.swapaxes(x_proj, 0, 1))
            return jnp.swapaxes(hs, 0, 1)
        key = jax.random.key(seed)
        ks = jax.random.split(key, 9)
        s = 1.0 / np.sqrt(H)
        u = lambda k, shape: jax.random.uniform(k, shape, jnp.float32, -s, s)
        return {'x': jax.random.normal(ks[0], (B, T, D), jnp.float32), 'W_ih': u(ks[1], (4 * H, D)), 'W_hh': u(ks[2], (4 * H, H)), 'b_ih': u(ks[3], (4 * H,)), 'b_hh': u(ks[4], (4 * H,)), 'W_lin': u(ks[5], (L, H)), 'b_lin': u(ks[6], (L,)), 'fw_att': jnp.full((1, H), 0.001, jnp.float32), 'bw_att': jnp.full((1, H), 0.001, jnp.float32)}
    _L0_ffn_all = _L0_ffn_setup()
    _L0_ffn_in = {k: v for k, v in _L0_ffn_all.items() if k in ('W_ih', 'W_hh', 'b_ih', 'b_hh', 'W_lin', 'b_lin', 'fw_att', 'bw_att')}
    del _L0_ffn_all
    return {'x': x, 'adj': adj, 'L0_gnn_item_feat': _L0_gnn_in['item_feat'], 'L0_gnn_W_item': _L0_gnn_in['W_item'], 'L0_gnn_b_item': _L0_gnn_in['b_item'], 'L0_gnn_W_user': _L0_gnn_in['W_user'], 'L0_gnn_b_user': _L0_gnn_in['b_user'], 'L0_ffn_W_ih': _L0_ffn_in['W_ih'], 'L0_ffn_W_hh': _L0_ffn_in['W_hh'], 'L0_ffn_b_ih': _L0_ffn_in['b_ih'], 'L0_ffn_b_hh': _L0_ffn_in['b_hh'], 'L0_ffn_W_lin': _L0_ffn_in['W_lin'], 'L0_ffn_b_lin': _L0_ffn_in['b_lin'], 'L0_ffn_fw_att': _L0_ffn_in['fw_att'], 'L0_ffn_bw_att': _L0_ffn_in['bw_att']}

def reference(x, adj, L0_gnn_item_feat, L0_gnn_W_item, L0_gnn_b_item, L0_gnn_W_user, L0_gnn_b_user, L0_ffn_W_ih, L0_ffn_W_hh, L0_ffn_b_ih, L0_ffn_b_hh, L0_ffn_W_lin, L0_ffn_b_lin, L0_ffn_fw_att, L0_ffn_bw_att):
    import jax
    import jax.numpy as jnp

    def _L0_gnn_ref(user_feat, item_feat, adj, W_item, b_item, W_user, b_user):
        import jax, jax.numpy as jnp
        import numpy as np
        N_USER = 10000
        N_ITEM = 10000
        HID = 128
        h = item_feat @ W_item.T + b_item
        b = user_feat @ W_user.T + b_user
        return jax.nn.relu(adj @ h + b)

    def _L0_ffn_ref(x, W_ih, W_hh, b_ih, b_hh, W_lin, b_lin, fw_att, bw_att):
        import jax, jax.numpy as jnp
        import numpy as np
        B, T, D, H, L = (16, 2048, 128, 128, 2)

        def _lstm(x, W_ih, W_hh, b_ih, b_hh):
            x_proj = jnp.einsum('btd,gd->btg', x, W_ih) + b_ih + b_hh
            h0 = jnp.zeros((x.shape[0], W_hh.shape[1]), x.dtype)
            c0 = jnp.zeros_like(h0)

            def step(carry, xp):
                h, c = carry
                gates = xp + h @ W_hh.T
                i, f, g, o = jnp.split(gates, 4, axis=-1)
                c = jax.nn.sigmoid(f) * c + jax.nn.sigmoid(i) * jnp.tanh(g)
                h = jax.nn.sigmoid(o) * jnp.tanh(c)
                return ((h, c), h)
            _, hs = jax.lax.scan(step, (h0, c0), jnp.swapaxes(x_proj, 0, 1))
            return jnp.swapaxes(hs, 0, 1)
        lstm_out = _lstm(x, W_ih, W_hh, b_ih, b_hh)
        logits = jnp.einsum('bth,lh->btl', lstm_out, W_lin) + b_lin
        g = jax.lax.stop_gradient(jnp.argmax(logits, axis=-1).astype(lstm_out.dtype))[..., None]
        w = g * lstm_out
        inc = jnp.cumsum(w, axis=1)
        prefix = inc - w
        suffix = inc[:, -1:, :] - inc
        return 2.0 * lstm_out + prefix * fw_att + suffix * bw_att
    x = x + _L0_gnn_ref(_layernorm(x, axis=-1), L0_gnn_item_feat, adj, L0_gnn_W_item, L0_gnn_b_item, L0_gnn_W_user, L0_gnn_b_user)
    x = x + _L0_ffn_ref(_layernorm(x, axis=-1)[None], L0_ffn_W_ih, L0_ffn_W_hh, L0_ffn_b_ih, L0_ffn_b_hh, L0_ffn_W_lin, L0_ffn_b_lin, L0_ffn_fw_att, L0_ffn_bw_att)[0]
    return x

_drawn_inputs = setup_inputs


def setup_inputs(seed=0):
    import zlib

    import numpy as np

    out = dict(_drawn_inputs(seed))
    spreads = {'L0_ffn_fw_att': (0.0010000000474974513, 0.6),
     'L0_ffn_bw_att': (0.0010000000474974513, 0.6)}
    factors = {}
    for name, (base, spread) in spreads.items():
        noise = np.random.default_rng([zlib.crc32(name.encode()), seed]).standard_normal(out[name].shape)
        drawn = base * np.exp(spread * noise) if base else spread * noise
        out[name] = jnp.asarray(drawn.astype(out[name].dtype))
    for name, factor in factors.items():
        out[name] = (out[name] * factor).astype(out[name].dtype)
    return out
```

```python
from contextlib import ExitStack

import concourse.bass as bass
from concourse import mybir

P = 128
N = 10000
HID = 128
NB = 20
BW = N // NB
CH = N // P
TAIL = N - CH * P
PIECES = 12
SLOTS = 4
SIZES = [CH // PIECES + (r < CH % PIECES) for r in range(PIECES)]
STARTS = [sum(SIZES[:r]) for r in range(PIECES)]
MAXC = max(SIZES)
SUB = 4
SW = BW // SUB
EPS = 1e-5
HANDOVER_TOL = 2.0 ** -19
GB = [0, 11, 17, NB]
K = [55, 100, 60]
W = [56, 50, 48]
T = [(GB[g + 1] - GB[g]) * BW for g in range(3)]
L = [T[g] // K[g] for g in range(3)]
STEPS = [W[g] + L[g] for g in range(3)]
OFF = [sum(W[:g + 1]) for g in range(3)]
FIRST_STEP = [sum(STEPS[:g]) for g in range(3)]
UHW = N + sum(W)
AT = dict(relu=1, x1=3, centre2=6, copy2=8, square2=9, var2=12, eps2=13, rstd2=14, diag2=18,
          bcast2=22, norm2=24, plus2=25, centre1=30, copy1=32, square1=33, var1=36, eps1=37,
          rstd1=38, diag1=42, bcast1=46, norm1=48)
STORE_AT = 10
A_BLOCKS = (12, 18)
A_SLOTS = [3 * i + 2 for i in range(26)]
B_SLOTS = [-1] + [2 * i + 1 for i in range(39)]
assert STEPS[0] == 6 * len(A_SLOTS) and STEPS[1] == 2 * len(B_SLOTS)


def group_of(block):
    return max(g for g in range(3) if GB[g] <= block)


def program(nc, xT, itemT, adj_main, adj_tail, w_itemT, b_item, w_userT, b_user, w_ihT, w_hhT,
            b_ih, b_hh, w_linT, b_lin, fw, bw, out):
    f32 = mybir.dt.float32
    i32 = mybir.dt.int32
    ALU = mybir.AluOpType
    ACT = mybir.ActivationFunctionType
    ds = bass.ds

    x1_dram = nc.dram_tensor("x1_copy", (P, N), f32).ap()
    u_dram = nc.dram_tensor("u_copy", (P, N), f32).ap()

    ctx = ExitStack()
    with ctx:
        def sb(name, shape, dt=f32):
            return ctx.enter_context(nc.sbuf_tensor(name, shape, dt))

        def sem(name):
            return ctx.enter_context(nc.semaphore(name))

        x1 = sb("x1", [P, N])
        uh = sb("uh", [P, UHW])
        hitem = sb("hitem", [P, (CH + 1) * HID])
        ring = sb("ring", [P, SLOTS, MAXC * BW])
        tail = sb("tail", [TAIL, BW])
        v = sb("v", [P, BW])
        xc = sb("xc", [P, BW])
        sq = sb("sq", [P, BW])
        un = sb("un", [P, BW])
        rl = un
        diag = sb("diag", [SW, SUB, SW])
        var = sb("var", [SW, SUB])
        rstd = sb("rstd", [SW, SUB])
        centre = sb("centre", [P, P])
        ident = sb("ident", [P, P])
        ones = sb("ones", [P, P])
        mean_col = sb("mean_col", [P, 1])
        minus_half = sb("minus_half", [P, 1])
        inv_rows = sb("inv_rows", [2, P])
        wi = sb("wi", [P, HID])
        wu = sb("wu", [P, HID])
        bi = sb("bi", [P, HID])
        bu = sb("bu", [P, 1])
        wx_raw = sb("wx_raw", [P, 4 * HID])
        wx = sb("wx", [P, 4 * HID])
        wh = sb("wh", [P, 4 * HID])
        bb = sb("bb", [2, 4 * HID])
        wl = sb("wl", [P, 2])
        bl = sb("bl", [P, 2])
        wd = sb("wd", [P, HID])
        wdc = sb("wdc", [P, 1])
        thr0 = sb("thr0", [P, 1])
        thr = sb("thr", [P, 1])
        fwc = sb("fwc", [P, 1])
        bwc = sb("bwc", [P, 1])
        hbw = sb("hbw", [P, 1])
        fmb = sb("fmb", [P, 1])
        mfw = sb("mfw", [P, 1])
        KM = max(K)
        gt = sb("gt", [P, 4 * KM])
        fc = sb("fc", [P, KM])
        ig = sb("ig", [P, KM])
        C = sb("C", [P, KM])
        H = sb("H", [P, KM])
        th = sb("th", [P, KM])
        H0 = sb("H0", [P, KM])
        C0 = sb("C0", [P, KM])
        Hend = sb("Hend", [P, 1])
        Cend = sb("Cend", [P, 1])
        dif = sb("dif", [P, 2 * KM + 2])
        okmin = sb("okmin", [P, 3])
        okall = sb("okall", [P, 1])
        flag = sb("flag", [P, 1], i32)
        w_g = sb("w_g", [P, BW])
        inc = sb("inc", [P, BW])
        carry = sb("carry", [P, 1])
        total = sb("total", [P, 1])

        psG = ctx.enter_context(nc.psum_tensor("psG", [P, 2, 512], f32))
        psL = ctx.enter_context(nc.psum_tensor("psL", [P, 2, 512], f32))
        psO = ctx.enter_context(nc.psum_tensor("psO", [P, 2, 512], f32))
        psN = ctx.enter_context(nc.psum_tensor("psN", [P, 512], f32))
        psD = ctx.enter_context(nc.psum_tensor("psD", [P, 512], f32))

        w_in = sem("w_in")
        x_in0 = sem("x_in0")
        x_in1 = sem("x_in1")
        item_in = sem("item_in")
        adj_in = [sem(f"adj_in{s}") for s in range(SLOTS)]
        tail_in = sem("tail_in")
        tail_used = sem("tail_used")
        adj_used = sem("adj_used")
        x1_stored = sem("x1_stored")
        u_stored = sem("u_stored")
        const_ready = sem("const_ready")
        wx_psum = sem("wx_psum")
        prep = sem("prep")
        item_psum = sem("item_psum")
        item_ready = sem("item_ready")
        v_ready = sem("v_ready")
        v_used = sem("v_used")
        relu_done = sem("relu_done")
        x1_ready = sem("x1_ready")
        ln_centred = sem("ln_centred")
        ln_copied = sem("ln_copied")
        ln_squared = sem("ln_squared")
        ln_var = sem("ln_var")
        ln_eps = sem("ln_eps")
        ln_rstd = sem("ln_rstd")
        ln_diag = sem("ln_diag")
        ln_bcast = sem("ln_bcast")
        ln_out = sem("ln_out")
        u_ready = sem("u_ready")
        halo_ready = sem("halo_ready")
        z_ifg = sem("z_ifg")
        z_o = sem("z_o")
        t_ifg = sem("t_ifg")
        t_o = sem("t_o")
        th_ready = sem("th_ready")
        parts = sem("parts")
        c_ready = sem("c_ready")
        h_ready = sem("h_ready")
        h_saved = sem("h_saved")
        bound = sem("bound")
        dchain = sem("dchain")
        d_ready = sem("d_ready")
        t1_ready = sem("t1_ready")
        fstep = sem("fstep")
        fin_done = sem("fin_done")
        ok_ready = sem("ok_ready")
        ok_sum = sem("ok_sum")
        flag_ready = sem("flag_ready")
        g_in = sem("g_in")
        g_init = sem("g_init")
        g_z = sem("g_z")
        g_t = sem("g_t")
        g_parts = sem("g_parts")
        g_c = sem("g_c")
        g_th = sem("g_th")
        g_h = sem("g_h")
        g_copy = sem("g_copy")
        g_d = sem("g_d")
        g_t1 = sem("g_t1")
        g_f = sem("g_f")
        g_fin = sem("g_fin")
        out_ready = sem("out_ready")
        out_done = sem("out_done")

        N_WEIGHTS = 14
        X0 = BW
        QUADS = (CH + 1 + 3) // 4

        def item_rows(c):
            return P if c < CH else TAIL

        def ring_col(c):
            r = max(q for q in range(PIECES) if STARTS[q] <= c)
            return r, c - STARTS[r]

        def uh_steps(g, step):
            start = OFF[g] + GB[g] * BW - W[g] + step
            return uh[:, ds(start, K[g], L[g])]

        def slots_in(j_kind):
            return {"plain": [], "A": A_SLOTS, "B": B_SLOTS}[j_kind]

        block = ctx.enter_context(nc.Block())

        @block.sync
        def _(sp):
            sp.dma_start(uh[:, OFF[0]:OFF[0] + 2048], itemT[:, 0:2048]).then_inc(item_in, 16)
            sp.dma_start(uh[:, OFF[0] + 2048:OFF[0] + N], itemT[:, 2048:N]).then_inc(item_in, 16)

            def load_piece(j, r):
                sp.dma_start(ring[:, r % SLOTS, 0:SIZES[r] * BW],
                             adj_main[j, :, STARTS[r] * BW:(STARTS[r] + SIZES[r]) * BW])\
                    .then_inc(adj_in[r % SLOTS], 16)

            def store_block(j):
                g = group_of(j) if isinstance(j, int) else None
                sp.wait_ge(x1_ready, j + 1)
                sp.dma_start(x1_dram[:, ds(j * BW, BW)], x1[:, ds(j * BW, BW)]).then_inc(x1_stored, 16)
                return g

            def store_u(j, g):
                sp.wait_ge(u_ready, j + 1)
                sp.dma_start(u_dram[:, ds(j * BW, BW)], uh[:, ds(j * BW + OFF[g], BW)])\
                    .then_inc(u_stored, 16)

            def load_block(j, store_group, first=False):
                for r in range(PIECES):
                    if not (first and r < SLOTS):
                        sp.wait_ge(adj_used, PIECES * j + (r - SLOTS + 1))
                    load_piece(j, r)
                    if r == 0 and first:
                        sp.dma_start(tail[:, :], adj_tail[0]).then_inc(tail_in, 16)
                    if r == STORE_AT - 2 and j is not None:
                        if not (isinstance(j, int) and j == NB - 1):
                            sp.wait_ge(tail_used, j + 1)
                            sp.dma_start(tail[:, :], adj_tail[j + 1]).then_inc(tail_in, 16)
                    if r == STORE_AT and store_group is not None:
                        if not (isinstance(j, int) and j == 1):
                            sp.wait_ge(x1_stored, (j - 1) * 16)
                            sp.wait_ge(u_stored, (j - 1) * 16)
                        store_block(j - 1)
                        store_u(j - 1, store_group)

            load_block(0, None, first=True)
            load_block(1, 0)
            with nc.sync.Fori(2, GB[1] + 1) as j:
                load_block(j, 0)
            with nc.sync.Fori(GB[1] + 1, GB[2] + 1) as j:
                load_block(j, 1)
            for j in range(GB[2] + 1, NB):
                load_block(j, 2)
            sp.wait_ge(x1_stored, 16 * (NB - 1))
            sp.wait_ge(u_stored, 16 * (NB - 1))
            store_block(NB - 1)
            store_u(NB - 1, 2)
            sp.wait_ge(x1_stored, 16 * NB)
            sp.wait_ge(u_stored, 16 * NB)

            sp.wait_ge(flag_ready, 1)
            redo = sp.value_load(flag[0:1, 0:1], min_val=0, max_val=1)
            with sp.If(redo > 0):
                sp.dma_start(x1[:, :], x1_dram).then_inc(g_in, 16)
                sp.dma_start(hitem[:, 0:N], u_dram).then_inc(g_in, 16)
                sp.wait_ge(g_in, 32)
            for q in range(4):
                sp.wait_ge(out_ready, q + 1)
                sp.dma_start(out[:, q * N // 4:(q + 1) * N // 4], x1[:, q * N // 4:(q + 1) * N // 4])\
                    .then_inc(out_done, 16)
            sp.wait_ge(out_done, 64)

        @block.gpsimd
        def _(pool):
            pool.memset(ident[:, :], 0.0).then_inc(const_ready, 1)
            pool.memset(centre[:, :], -1.0 / HID).then_inc(const_ready, 1)
            pool.memset(ones[:, :], 1.0).then_inc(const_ready, 1)
            pool.memset(mean_col[:, :], 1.0 / HID).then_inc(const_ready, 1)
            pool.memset(minus_half[:, :], -0.5).then_inc(const_ready, 1)
            pool.memset(inv_rows[:, :], 1.0 / HID).then_inc(const_ready, 1)
            pool.memset(uh[:, 0:OFF[0]], 0.0).then_inc(const_ready, 1)
            pool.wait_ge(const_ready, 7)
            for m, d in ((ident, 1.0), (centre, 1.0 - 1.0 / HID)):
                pool.affine_select(out=m[:, :], in_=m[:, :], compare_op=ALU.not_equal, fill=d,
                                   base=0, pattern=[[-1, P]], channel_multiplier=1)\
                    .then_inc(const_ready, 1)

            def square(m):
                pool.wait_ge(ln_copied, m + 1)
                pool.tensor_tensor(sq[:, :], xc[:, :], xc[:, :], ALU.mult).then_inc(ln_squared, 1)

            def inv_std(m):
                pool.wait_ge(ln_eps, m + 1)
                pool.tensor_tensor(rstd[:, :], var[:, :], minus_half[0:SW, :].to_broadcast([SW, SUB]),
                                   ALU.pow).then_inc(ln_rstd, 1)

            def plus_one(j, g):
                pool.wait_ge(ln_out, j + 1)
                pool.tensor_tensor(uh[:, ds(j * BW + OFF[g], BW)], un[:, :],
                                   ones[:, 0:1].to_broadcast([P, BW]), ALU.add)\
                    .then_inc(u_ready, 1)

            def t1(f, g, n):
                pool.wait_ge(h_saved, n)
                pool.tensor_tensor(x1[:, f * BW:(f + 1) * BW], x1[:, f * BW:(f + 1) * BW],
                                   uh[:, OFF[g] + f * BW:OFF[g] + (f + 1) * BW], ALU.add).then_inc(t1_ready, 1)

            square(0)
            inv_std(0)
            square(1)
            inv_std(1)

            def body(j, g, both=True):
                square(2 * j)
                inv_std(2 * j)
                plus_one(j - 1, g)
                if both:
                    square(2 * j + 1)
                    inv_std(2 * j + 1)

            with nc.gpsimd.Fori(1, GB[1] + 1) as j:
                body(j, 0)
            with nc.gpsimd.Fori(GB[1] + 1, GB[2] + 1) as j:
                body(j, 1)
            body(NB - 2, 2)
            body(NB - 1, 2, both=False)
            square(2 * NB - 1)
            inv_std(2 * NB - 1)
            plus_one(NB - 1, 2)
            pool.wait_ge(x1_stored, 16 * NB)
            for f in range(NB):
                t1(f, group_of(f), L[0] + L[1] + L[2])

            pool.wait_ge(flag_ready, 1)
            redo = pool.value_load(flag[0:1, 0:1], min_val=0, max_val=1)
            with pool.If(redo > 0):
                pool.wait_ge(g_copy, N)
                for g in range(3):
                    with nc.gpsimd.Fori(GB[g], GB[g + 1]) as f:
                        pool.tensor_tensor(x1[:, ds(f * BW, BW)], x1[:, ds(f * BW, BW)],
                                           uh[:, ds(f * BW + OFF[g], BW)], ALU.add).then_inc(g_t1, 1)

        @block.scalar
        def _(act):
            act.dma_start(wi[:, :], w_itemT).then_inc(w_in, 16)
            act.dma_start(bi[:, :], b_item[0:1, :].to_broadcast([P, HID])).then_inc(w_in, 16)
            act.dma_start(x1[:, 0:X0], xT[:, 0:X0]).then_inc(x_in0, 16)
            act.dma_start(wu[:, :], w_userT).then_inc(w_in, 16)
            act.dma_start(bu[:, :], b_user).then_inc(w_in, 16)
            act.dma_start(wx_raw[:, :], w_ihT).then_inc(w_in, 16)
            act.dma_start(wh[:, :], w_hhT).then_inc(w_in, 16)
            act.dma_start(bb[0:1, :], b_ih).then_inc(w_in, 16)
            act.dma_start(bb[1:2, :], b_hh).then_inc(w_in, 16)
            act.dma_start(wl[:, :], w_linT).then_inc(w_in, 16)
            act.dma_start(bl[:, :], b_lin[0:1, :].to_broadcast([P, 2])).then_inc(w_in, 16)
            act.dma_start(fwc[:, :], fw).then_inc(w_in, 16)
            act.dma_start(bwc[:, :], bw).then_inc(w_in, 16)
            act.dma_start(x1[:, X0:N], xT[:, X0:N]).then_inc(x_in1, 16)

            def relu(j):
                act.wait_ge(adj_used, PIECES * (j + 1))
                if isinstance(j, int) and j == NB - 1:
                    act.wait_ge(u_ready, j)
                else:
                    act.wait_ge(v_ready, j + 2)
                nc.scalar.activation(rl[:, :], psG[:, j % 2, 0:BW], ACT.Relu, bias=bu[:, 0:1])\
                    .then_inc(relu_done, 1)

            def copy_centred(m, reader, count):
                act.wait_ge(ln_centred, m + 1)
                if reader is not None:
                    act.wait_ge(reader, count)
                nc.scalar.activation(xc[:, :], psN[:, 0:BW], ACT.Copy).then_inc(ln_copied, 1)

            def lstm(g, n, par):
                k = K[g]
                act.wait_ge(z_ifg, n + 1)
                nc.scalar.activation(gt[:, 0:3 * k], psL[:, par, 0:3 * k], ACT.Tanh).then_inc(t_ifg, 1)
                act.wait_ge(z_o, n + 1)
                nc.scalar.activation(gt[:, 3 * k:4 * k], psO[:, par, 0:k], ACT.Tanh).then_inc(t_o, 1)
                act.wait_ge(c_ready, n + 1)
                nc.scalar.activation(th[:, 0:k], C[:, 0:k], ACT.Tanh, scale=0.5).then_inc(th_ready, 1)

            def body(j, kind, step0, has2=True, has1=True):
                g = {"plain": 0, "A": 0, "B": 1}[kind]
                slots = slots_in(kind)
                for c in range(-1, CH):
                    if has2 and c == AT["relu"]:
                        relu(j - 1)
                    if has2 and c == AT["copy2"]:
                        copy_centred(2 * j, v_ready, j + 1)
                    if has1 and c == AT["copy1"]:
                        copy_centred(2 * j + 1, ln_out if has2 else v_ready, j if has2 else 1)
                    if c in slots:
                        i = slots.index(c)
                        lstm(g, step0 + i, i % 2)

            copy_centred(0, None, 0)
            body(0, "plain", 0, has2=False)
            with nc.scalar.Fori(1, A_BLOCKS[0]) as j:
                body(j, "plain", 0)
            with nc.scalar.Fori(A_BLOCKS[0], A_BLOCKS[1]) as j:
                body(j, "A", (j - A_BLOCKS[0]) * len(A_SLOTS))
            body(NB - 2, "B", FIRST_STEP[1])
            body(NB - 1, "B", FIRST_STEP[1] + len(B_SLOTS), has1=False)
            relu(NB - 1)
            copy_centred(2 * NB - 1, ln_out, NB - 1)
            with nc.scalar.Fori(0, STEPS[2] // 2) as i:
                lstm(2, FIRST_STEP[2] + 2 * i, 0)
                lstm(2, FIRST_STEP[2] + 2 * i + 1, 1)
            if STEPS[2] % 2:
                lstm(2, FIRST_STEP[2] + STEPS[2] - 1, 0)

            act.wait_ge(flag_ready, 1)
            redo = act.value_load(flag[0:1, 0:1], min_val=0, max_val=1)
            with act.If(redo > 0):
                with nc.scalar.Fori(0, N) as t:
                    act.wait_ge(g_z, t + 1)
                    nc.scalar.activation(gt[:, 0:4], psL[:, 0, 0:4], ACT.Tanh).then_inc(g_t, 1)
                    act.wait_ge(g_c, t + 1)
                    nc.scalar.activation(th[:, 0:1], C[:, 0:1], ACT.Tanh, scale=0.5).then_inc(g_th, 1)

        @block.tensor
        def _(pe):
            def centre_rows(j, reader, count):
                if reader is not None:
                    pe.wait_ge(reader, count)
                pe.matmul(psN[:, 0:BW], centre[:, :], x1[:, ds(j * BW, BW)], start=True, stop=True)\
                    .then_inc(ln_centred, 1)

            def variance(m):
                pe.wait_ge(ln_squared, m + 1)
                for s in range(SUB):
                    last = pe.matmul(psN[0:SW, s:s + 1], sq[:, s * SW:(s + 1) * SW], mean_col[:, :],
                                     start=True, stop=True)
                last.then_inc(ln_var, 1)

            def broadcast(m):
                pe.wait_ge(ln_diag, m + 1)
                pe.matmul(psN[:, 0:BW], ones[0:SW, :], diag[:, :, :].rearrange("p s w -> p (s w)"),
                          start=True, stop=True).then_inc(ln_bcast, 1)

            def lstm(g, n, step, par, early=False):
                k = K[g]
                if early:
                    pe.wait_ge(h_ready, n + g + 1)
                else:
                    pe.wait_ge(t_o, n - 1)
                def gate(q):
                    return psL[:, par, q * k:(q + 1) * k] if q < 3 else psO[:, par, 0:k]

                for q in range(4):
                    pe.matmul(gate(q), wx[:, q * HID:(q + 1) * HID], uh_steps(g, step),
                              start=(q in (0, 3)), stop=False, skip_group_check=True)
                pe.wait_ge(h_ready, n + g + 1)
                for q in (0, 1, 2, 3):
                    last = pe.matmul(gate(q), wh[:, q * HID:(q + 1) * HID], H[:, 0:k], start=False, stop=True, skip_group_check=True)
                    if q == 2:
                        last.then_inc(z_ifg, 1)
                last.then_inc(z_o, 1)

            def body(j, kind, step0, has2=True, has1=True):
                g = {"plain": 0, "A": 0, "B": 1}[kind]
                slots = slots_in(kind)

                def slot(c):
                    if c in slots:
                        i = slots.index(c)
                        lstm(g, FIRST_STEP[g] + step0 + i, step0 + i, i % 2, early=(i < 2))

                slot(-1)
                pe.wait_ge(tail_in, 16 * (j + 1))
                pe.wait_ge(v_ready, j + 1)
                pe.matmul(psG[:, j % 2, 0:BW], wu[:, :], v[:, :], start=True, stop=False).then_inc(v_used, 1)
                pe.matmul(psG[:, j % 2, 0:BW], hitem[0:TAIL, CH * HID:(CH + 1) * HID], tail[:, :],
                          start=False, stop=False).then_inc(tail_used, 1)
                for c in range(CH):
                    r, i = ring_col(c)
                    if i == 0:
                        pe.wait_ge(adj_in[r % SLOTS], 16 * (PIECES // SLOTS * j + r // SLOTS + 1))
                    mm = pe.matmul(psG[:, j % 2, 0:BW], hitem[:, c * HID:(c + 1) * HID],
                                   ring[:, r % SLOTS, i * BW:(i + 1) * BW], start=False, stop=(c == CH - 1))
                    if i == SIZES[r] - 1:
                        mm.then_inc(adj_used, 1)
                    if has2 and c == AT["centre2"]:
                        pe.wait_ge(x1_ready, j)
                        centre_rows(j - 1, v_ready, j + 1)
                    if has2 and c == AT["var2"]:
                        variance(2 * j)
                    if has2 and c == AT["bcast2"]:
                        broadcast(2 * j)
                    if has1 and c == AT["centre1"]:
                        centre_rows(j + 1, ln_out if has2 else v_ready, j if has2 else 1)
                    if has1 and c == AT["var1"]:
                        variance(2 * j + 1)
                    if has1 and c == AT["bcast1"]:
                        broadcast(2 * j + 1)
                    slot(c)

            pe.wait_ge(const_ready, 9)
            pe.wait_ge(x_in0, 16)
            centre_rows(0, None, 0)
            pe.wait_ge(w_in, 16 * 12)
            pe.wait_ge(item_in, 32)
            for q in range(QUADS):
                if q >= 2:
                    pe.wait_ge(item_ready, q - 1)
                for c in range(4 * q, min(4 * q + 4, CH + 1)):
                    rows = item_rows(c)
                    last = pe.matmul(psL[0:rows, q % 2, (c % 4) * HID:(c % 4 + 1) * HID],
                                     uh[:, OFF[0] + c * P:OFF[0] + c * P + rows], wi[:, :],
                                     start=True, stop=True)
                last.then_inc(item_psum, 1)
                if q == 2:
                    variance(0)
                if q == 6:
                    broadcast(0)
            pe.wait_ge(item_ready, QUADS - 1)
            pe.matmul(psD[:, :], centre[:, :], wx_raw[:, :], start=True, stop=False)
            pe.matmul(psD[:, :], inv_rows[:, :], bb[:, :], start=False, stop=True).then_inc(wx_psum, 1)
            pe.wait_ge(item_ready, QUADS + 1)
            pe.wait_ge(x_in1, 16)

            body(0, "plain", 0, has2=False)
            with nc.tensor.Fori(1, A_BLOCKS[0]) as j:
                body(j, "plain", 0)
            pe.wait_ge(prep, 15)
            with nc.tensor.Fori(A_BLOCKS[0], A_BLOCKS[1]) as j:
                body(j, "A", (j - A_BLOCKS[0]) * len(A_SLOTS))
            pe.wait_ge(halo_ready, 2)
            body(NB - 2, "B", 0)
            body(NB - 1, "B", len(B_SLOTS), has1=False)
            pe.wait_ge(x1_ready, NB)
            centre_rows(NB - 1, ln_out, NB - 1)
            variance(2 * NB - 1)
            broadcast(2 * NB - 1)
            pe.wait_ge(u_ready, NB)
            with nc.tensor.Fori(0, STEPS[2] // 2) as i:
                lstm(2, FIRST_STEP[2] + 2 * i, 2 * i, 0)
                lstm(2, FIRST_STEP[2] + 2 * i + 1, 2 * i + 1, 1)
            if STEPS[2] % 2:
                lstm(2, FIRST_STEP[2] + STEPS[2] - 1, STEPS[2] - 1, 0)

            pe.wait_ge(prep, 15)
            pe.wait_ge(h_saved, sum(L))
            for f in range(NB):
                g = group_of(f)
                if f:
                    pe.wait_ge(fin_done, 5 * f - 4)
                pe.matmul(psD[:, 0:BW], wd[:, :], uh[:, OFF[g] + f * BW:OFF[g] + (f + 1) * BW],
                          start=True, stop=True).then_inc(d_ready, 1)
            pe.wait_ge(ok_ready, 1)
            pe.matmul(psN[:, 0:1], ones[:, :], okall[:, :], start=True, stop=True).then_inc(ok_sum, 1)

            pe.wait_ge(flag_ready, 1)
            redo = pe.value_load(flag[0:1, 0:1], min_val=0, max_val=1)
            with pe.If(redo > 0):
                pe.wait_ge(g_in, 32)
                with nc.tensor.Fori(0, N) as t:
                    pe.wait_ge(g_h, t + 1)
                    for q in range(4):
                        pe.matmul(psL[:, 0, q:q + 1], wx[:, q * HID:(q + 1) * HID], hitem[:, ds(t, 1)],
                                  start=True, stop=False)
                        last = pe.matmul(psL[:, 0, q:q + 1], wh[:, q * HID:(q + 1) * HID], H[:, 0:1],
                                         start=False, stop=True)
                    last.then_inc(g_z, 1)
                pe.wait_ge(g_copy, N)
                for g in range(3):
                    with nc.tensor.Fori(GB[g], GB[g + 1]) as f:
                        pe.wait_ge(g_f, 5 * f + 1)
                        pe.matmul(psD[:, 0:BW], wd[:, :], uh[:, ds(f * BW + OFF[g], BW)],
                                  start=True, stop=True).then_inc(g_d, 1)

        @block.vector
        def _(dve):
            dve.memset(C[:, :], 0.0).then_inc(prep, 1)
            dve.memset(H[:, :], 0.0).then_inc(h_ready, 1)
            dve.memset(carry[:, :], 0.0).then_inc(prep, 1)

            def eps(m):
                dve.wait_ge(ln_var, m + 1)
                dve.tensor_scalar(var[:, :], psN[0:SW, 0:SUB], EPS, None, ALU.add).then_inc(ln_eps, 1)

            def diagonal(m):
                dve.wait_ge(ln_rstd, m + 1)
                dve.tensor_tensor(diag[:, :, :], ident[0:SW, 0:SW].unsqueeze(1).to_broadcast([SW, SUB, SW]),
                                  rstd[:, :].unsqueeze(2).to_broadcast([SW, SUB, SW]), ALU.mult)\
                    .then_inc(ln_diag, 1)

            def norm1(m, j):
                dve.wait_ge(ln_bcast, m + 1)
                if not (isinstance(j, int) and j == 0):
                    dve.wait_ge(v_used, j)
                dve.tensor_tensor(v[:, :], xc[:, :], psN[:, 0:BW], ALU.mult).then_inc(v_ready, 1)

            def norm2(m):
                dve.wait_ge(ln_bcast, m + 1)
                dve.tensor_tensor(un[:, :], xc[:, :], psN[:, 0:BW], ALU.mult).then_inc(ln_out, 1)

            def add_relu(j):
                dve.wait_ge(relu_done, j + 1)
                dve.tensor_tensor(x1[:, ds(j * BW, BW)], x1[:, ds(j * BW, BW)], rl[:, :], ALU.add)\
                    .then_inc(x1_ready, 1)

            def lstm(g, n, step, kind):
                k = K[g]
                dve.wait_ge(t_ifg, n + 1)
                dve.scalar_tensor_tensor(fc[:, 0:k], gt[:, k:2 * k], 1.0, C[:, 0:k], ALU.add, ALU.mult)\
                    .then_inc(parts, 1)
                dve.scalar_tensor_tensor(ig[:, 0:k], gt[:, 0:k], 1.0, gt[:, 2 * k:3 * k], ALU.add, ALU.mult)\
                    .then_inc(parts, 1)
                dve.wait_ge(parts, 2 * n + 2)
                dve.scalar_tensor_tensor(C[:, 0:k], fc[:, 0:k], 0.5, ig[:, 0:k], ALU.mult, ALU.add)\
                    .then_inc(c_ready, 1)
                dve.wait_ge(t_o, n + 1)
                dve.wait_ge(th_ready, n + 1)
                h_step = dve.scalar_tensor_tensor(H[:, 0:k], gt[:, 3 * k:4 * k], 1.0, th[:, 0:k],
                                                  ALU.add, ALU.mult)
                if kind == "boundary":
                    h_step.then_inc(bound, 1)
                    dve.wait_ge(bound, g + 1)
                    if g == 0:
                        dve.memset(C[:, 0:1], 0.0).then_inc(dchain, 1)
                        dve.memset(H[:, 0:1], 0.0).then_inc(h_ready, 1)
                        dve.wait_ge(dchain, 1)
                        dve.wait_ge(h_ready, n + g + 2)
                    dve.tensor_copy(C0[:, 0:k], C[:, 0:k]).then_inc(dchain, 1)
                    save = dve.tensor_copy(H0[:, 0:k], H[:, 0:k])
                    save.then_inc(dchain if g == 0 else h_ready, 1)
                else:
                    h_step.then_inc(h_ready, 1)
                if kind == "main":
                    dve.wait_ge(h_ready, n + g + 2)
                    dve.tensor_copy(uh_steps(g, step), H[:, 0:k]).then_inc(h_saved, 1)

            def compare(g, last_step):
                k = K[g]
                dve.wait_ge(c_ready, last_step + 1)
                dve.wait_ge(h_ready, last_step + g + 2)
                dve.wait_ge(dchain, 3 + g)
                n = 0
                pairs = [(H[:, 0:k - 1], H0[:, 1:k]), (C[:, 0:k - 1], C0[:, 1:k])]
                if g:
                    pairs += [(Hend[:, :], H0[:, 0:1]), (Cend[:, :], C0[:, 0:1])]

                def link(ins):
                    ins.then_inc(fstep, 1)
                    fcount[0] += 1

                for a, b in pairs:
                    w = a.shape[1]
                    link(dve.tensor_tensor(dif[:, n:n + w], a, b, ALU.subtract))
                    n += w
                dve.wait_ge(fstep, fcount[0])
                link(dve.tensor_tensor(dif[:, 0:n], dif[:, 0:n], dif[:, 0:n], ALU.mult))
                dve.wait_ge(fstep, fcount[0])
                link(dve.tensor_scalar(dif[:, 0:n], dif[:, 0:n], HANDOVER_TOL ** 2, None, ALU.is_le))
                dve.wait_ge(fstep, fcount[0])
                link(dve.tensor_reduce(okmin[:, g:g + 1], dif[:, 0:n], mybir.AxisListType.X, ALU.min))
                link(dve.tensor_copy(Hend[:, :], H[:, k - 1:k]))
                link(dve.tensor_copy(Cend[:, :], C[:, k - 1:k]))
                dve.wait_ge(fstep, fcount[0])
                if g < 2:
                    dve.memset(C[:, :], 0.0).then_inc(fstep, 1)
                    fcount[0] += 1
                    dve.wait_ge(fstep, fcount[0])
                    dve.memset(H[:, :], 0.0).then_inc(h_ready, 1)

            fcount = [0]

            def body(j, kind, step0, has2=True, has1=True, kinds=None):
                g = {"plain": 0, "A": 0, "B": 1}[kind]
                slots = slots_in(kind)
                for c in range(-1, CH):
                    if has2 and c == AT["x1"]:
                        add_relu(j - 1)
                    if has2 and c == AT["eps2"]:
                        eps(2 * j)
                    if has2 and c == AT["diag2"]:
                        diagonal(2 * j)
                    if has2 and c == AT["norm2"]:
                        norm2(2 * j)
                    if has1 and c == AT["eps1"]:
                        eps(2 * j + 1)
                    if has1 and c == AT["diag1"]:
                        diagonal(2 * j + 1)
                    if has1 and c == AT["norm1"]:
                        norm1(2 * j + 1, j + 1)
                    if c in slots:
                        i = slots.index(c)
                        lstm(g, FIRST_STEP[g] + step0 + i, step0 + i, kinds(i))

            dve.wait_ge(w_in, 16 * 12)
            dve.wait_ge(const_ready, 9)

            def item_copy(q):
                dve.wait_ge(item_psum, q + 1)
                for c0, c1, rows in ([(4 * q, min(4 * q + 4, CH), P)] + ([(CH, CH + 1, TAIL)] if q == QUADS - 1 else [])):
                    n = c1 - c0
                    a = (c0 % 4) * HID
                    last = dve.tensor_tensor(
                        hitem[0:rows, c0 * HID:c1 * HID].rearrange("p (c h) -> p c h", h=HID),
                        psL[0:rows, q % 2, a:a + n * HID].rearrange("p (c h) -> p c h", h=HID),
                        bi[0:rows, :].unsqueeze(1).to_broadcast([rows, n, HID]), ALU.add)
                    last.then_inc(item_ready, 1)

            for q in range(QUADS):
                item_copy(q)
                if q == 2:
                    eps(0)
                if q == 4:
                    diagonal(0)
                if q == 6:
                    norm1(0, 0)
            dve.wait_ge(wx_psum, 1)
            dve.tensor_scalar(wx[:, 0:2 * HID], psD[:, 0:2 * HID], 0.5, None, ALU.mult).then_inc(prep, 1)
            dve.tensor_scalar(wx[:, 2 * HID:3 * HID], psD[:, 2 * HID:3 * HID], 1.0, None, ALU.mult).then_inc(prep, 1)
            dve.tensor_scalar(wx[:, 3 * HID:4 * HID], psD[:, 3 * HID:4 * HID], 0.5, None, ALU.mult).then_inc(prep, 1)
            dve.tensor_scalar(wh[:, 0:2 * HID], wh[:, 0:2 * HID], 0.25, None, ALU.mult).then_inc(prep, 1)
            dve.tensor_scalar(wh[:, 2 * HID:3 * HID], wh[:, 2 * HID:3 * HID], 0.5, None, ALU.mult).then_inc(prep, 1)
            dve.tensor_scalar(wh[:, 3 * HID:4 * HID], wh[:, 3 * HID:4 * HID], 0.25, None, ALU.mult).then_inc(prep, 1)
            dve.tensor_tensor(wdc[:, :], wl[:, 1:2], wl[:, 0:1], ALU.subtract).then_inc(prep, 1)
            dve.tensor_tensor(thr0[:, :], bl[:, 0:1], bl[:, 1:2], ALU.subtract).then_inc(prep, 1)
            dve.tensor_scalar(mfw[:, :], fwc[:, :], -0.5, None, ALU.mult).then_inc(prep, 1)
            dve.tensor_scalar(hbw[:, :], bwc[:, :], 0.5, None, ALU.mult).then_inc(prep, 1)
            dve.wait_ge(prep, 12)
            dve.scalar_tensor_tensor(fmb[:, :], mfw[:, :], -1.0, hbw[:, :], ALU.mult, ALU.subtract).then_inc(prep, 1)
            dve.tensor_scalar(wd[:, :], ones[:, :], wdc[:, 0:1], None, ALU.mult).then_inc(prep, 1)
            dve.tensor_scalar(thr[:, :], thr0[:, :], 2.0, None, ALU.mult).then_inc(prep, 1)
            dve.wait_ge(prep, 15)

            body(0, "plain", 0, has2=False)
            with nc.vector.Fori(1, A_BLOCKS[0]) as j:
                body(j, "plain", 0)
            nA = len(A_SLOTS)
            mixed = A_BLOCKS[0] + W[0] // nA
            with nc.vector.Fori(A_BLOCKS[0], mixed) as j:
                body(j, "A", (j - A_BLOCKS[0]) * nA, kinds=lambda i: "run-in")
            e0 = OFF[0] + T[0]
            dve.wait_ge(u_ready, GB[1])
            dve.tensor_copy(uh[:, e0:e0 + W[1]], uh[:, e0 - W[1]:e0]).then_inc(halo_ready, 1)
            dve.wait_ge(halo_ready, 1)
            dve.wait_ge(u_stored, 16 * (mixed - 1))
            b0 = W[0] - (mixed - A_BLOCKS[0]) * nA
            body(mixed, "A", (mixed - A_BLOCKS[0]) * nA,
                 kinds=lambda i: "run-in" if i < b0 - 1 else "boundary" if i == b0 - 1 else "main")
            with nc.vector.Fori(mixed + 1, A_BLOCKS[1]) as j:
                body(j, "A", (j - A_BLOCKS[0]) * nA, kinds=lambda i: "main")
            compare(0, STEPS[0] - 1)
            e1 = OFF[1] + T[0] + T[1]
            dve.wait_ge(u_ready, GB[2])
            dve.tensor_copy(uh[:, e1:e1 + W[2]], uh[:, e1 - W[2]:e1]).then_inc(halo_ready, 1)
            body(NB - 2, "B", 0, kinds=lambda i: "run-in")
            dve.wait_ge(u_stored, 16 * GB[2])
            b1 = W[1] - len(B_SLOTS)
            body(NB - 1, "B", len(B_SLOTS), has1=False,
                 kinds=lambda i: "run-in" if i < b1 - 1 else "boundary" if i == b1 - 1 else "main")
            compare(1, STEPS[0] + STEPS[1] - 1)
            add_relu(NB - 1)
            eps(2 * NB - 1)
            diagonal(2 * NB - 1)
            norm2(2 * NB - 1)
            s2 = FIRST_STEP[2]
            pairs_in = (W[2] - 2) // 2
            with nc.vector.Fori(0, pairs_in) as i:
                lstm(2, s2 + 2 * i, 2 * i, "run-in")
                lstm(2, s2 + 2 * i + 1, 2 * i + 1, "run-in")
            lstm(2, s2 + W[2] - 2, W[2] - 2, "run-in")
            lstm(2, s2 + W[2] - 1, W[2] - 1, "boundary")
            dve.wait_ge(u_stored, 16 * NB)
            with nc.vector.Fori(W[2], STEPS[2]) as i:
                lstm(2, i + s2, i, "main")
            compare(2, sum(STEPS) - 1)
            dve.wait_ge(fstep, fcount[0])
            dve.tensor_reduce(okall[:, :], okmin[:, :], mybir.AxisListType.X, ALU.min).then_inc(ok_ready, 1)

            def finish(cols, hist, ready, t1, done, st, n0, f):
                if not (isinstance(n0, int) and n0 == 0):
                    dve.wait_ge(st, n0)
                dve.wait_ge(ready, f + 1)
                ins = dve.scalar_tensor_tensor(w_g[:, :], psD[:, 0:BW], thr[:, 0:1], hist, ALU.is_gt, ALU.mult)
                ins.then_inc(st, 1)
                dve.wait_ge(st, n0 + 1)
                dve.tensor_tensor_scan(inc[:, :], w_g[:, :], w_g[:, :], carry[:, 0:1], ALU.add, ALU.bypass)\
                    .then_inc(st, 1)
                dve.wait_ge(st, n0 + 2)
                dve.tensor_copy(carry[:, :], inc[:, BW - 1:BW]).then_inc(st, 1)
                dve.wait_ge(t1, f + 1)
                dve.scalar_tensor_tensor(cols, inc[:, :], fmb[:, 0:1], cols, ALU.mult, ALU.add).then_inc(st, 1)
                dve.wait_ge(st, n0 + 4)
                dve.scalar_tensor_tensor(cols, w_g[:, :], mfw[:, 0:1], cols, ALU.mult, ALU.add).then_inc(st, 1)

            for f in range(NB):
                g = group_of(f)
                finish(x1[:, f * BW:(f + 1) * BW], uh[:, OFF[g] + f * BW:OFF[g] + (f + 1) * BW],
                       d_ready, t1_ready, fin_done, fin_done, 5 * f, f)
            dve.wait_ge(ok_sum, 1)
            dve.wait_ge(fin_done, 5 * NB)
            dve.tensor_scalar(flag[:, :], psN[:, 0:1], float(P) - 0.5, None, ALU.is_lt).then_inc(flag_ready, 1)
            dve.wait_ge(flag_ready, 1)
            redo = dve.value_load(flag[0:1, 0:1], min_val=0, max_val=1)
            with dve.If(redo > 0):
                dve.memset(C[:, 0:1], 0.0).then_inc(g_init, 1)
                dve.memset(carry[:, :], 0.0).then_inc(g_f, 1)
                dve.wait_ge(g_init, 1)
                dve.wait_ge(g_f, 1)
                dve.memset(H[:, 0:1], 0.0).then_inc(g_h, 1)
                for g in range(3):
                    with nc.vector.Fori(GB[g] * BW, GB[g + 1] * BW) as t:
                        dve.wait_ge(g_t, t + 1)
                        dve.scalar_tensor_tensor(fc[:, 0:1], gt[:, 1:2], 1.0, C[:, 0:1], ALU.add, ALU.mult)\
                            .then_inc(g_parts, 1)
                        dve.scalar_tensor_tensor(ig[:, 0:1], gt[:, 0:1], 1.0, gt[:, 2:3], ALU.add, ALU.mult)\
                            .then_inc(g_parts, 1)
                        dve.wait_ge(g_parts, 2 * t + 2)
                        dve.scalar_tensor_tensor(C[:, 0:1], fc[:, 0:1], 0.5, ig[:, 0:1], ALU.mult, ALU.add)\
                            .then_inc(g_c, 1)
                        dve.wait_ge(g_th, t + 1)
                        dve.scalar_tensor_tensor(H[:, 0:1], gt[:, 3:4], 1.0, th[:, 0:1], ALU.add, ALU.mult)\
                            .then_inc(g_h, 1)
                        dve.wait_ge(g_h, t + 2)
                        dve.tensor_copy(uh[:, ds(t + OFF[g], 1)], H[:, 0:1]).then_inc(g_copy, 1)
                dve.wait_ge(g_copy, N)
                for g in range(3):
                    with nc.vector.Fori(GB[g], GB[g + 1]) as f:
                        finish(x1[:, ds(f * BW, BW)], uh[:, ds(f * BW + OFF[g], BW)],
                               g_d, g_t1, g_f, g_f, 5 * f + 1, f)
                dve.wait_ge(g_f, 5 * NB + 1)
            dve.tensor_tensor(total[:, :], carry[:, :], hbw[:, :], ALU.mult).then_inc(prep, 1)
            dve.wait_ge(prep, 16)
            for q in range(4):
                dve.tensor_scalar(x1[:, q * N // 4:(q + 1) * N // 4], x1[:, q * N // 4:(q + 1) * N // 4],
                                  total[:, 0:1], None, ALU.add).then_inc(out_ready, 1)


def kernel(x, adj, L0_gnn_item_feat, L0_gnn_W_item, L0_gnn_b_item, L0_gnn_W_user, L0_gnn_b_user,
           L0_ffn_W_ih, L0_ffn_W_hh, L0_ffn_b_ih, L0_ffn_b_hh, L0_ffn_W_lin, L0_ffn_b_lin,
           L0_ffn_fw_att, L0_ffn_bw_att):
    import numpy as np
    import concourse.bacc as bacc
    from concourse.bass_utils import run_bass_kernel_spmd

    adjT = np.asarray(adj).T
    main = adjT[:CH * P].reshape(CH, P, NB, BW).transpose(2, 1, 0, 3).reshape(NB, P, CH * BW)
    short = adjT[CH * P:].reshape(TAIL, NB, BW).transpose(1, 0, 2)
    host = [
        ("xT", np.asarray(x).T), ("itemT", np.asarray(L0_gnn_item_feat).T),
        ("adj_main", main), ("adj_tail", short),
        ("w_itemT", np.asarray(L0_gnn_W_item).T), ("b_item", np.asarray(L0_gnn_b_item).reshape(1, HID)),
        ("w_userT", np.asarray(L0_gnn_W_user).T), ("b_user", np.asarray(L0_gnn_b_user).reshape(HID, 1)),
        ("w_ihT", np.asarray(L0_ffn_W_ih).T), ("w_hhT", np.asarray(L0_ffn_W_hh).T),
        ("b_ih", np.asarray(L0_ffn_b_ih).reshape(1, 4 * HID)), ("b_hh", np.asarray(L0_ffn_b_hh).reshape(1, 4 * HID)),
        ("w_linT", np.asarray(L0_ffn_W_lin).T), ("b_lin", np.asarray(L0_ffn_b_lin).reshape(1, 2)),
        ("fw", np.asarray(L0_ffn_fw_att).reshape(HID, 1)), ("bw", np.asarray(L0_ffn_bw_att).reshape(HID, 1)),
    ]
    nc = bacc.Bacc("TRN2", target_bir_lowering=False, num_devices=1)
    arrays, args = {}, []
    for name, a in host:
        a = np.ascontiguousarray(a)
        arrays[f"in_{name}"] = a
        args.append(nc.dram_tensor(f"in_{name}", a.shape, mybir.dt.from_np(a.dtype), kind="ExternalInput").ap())
    out = nc.dram_tensor("out_0", (HID, N), mybir.dt.float32, kind="ExternalOutput").ap()
    program(nc, *args, out)
    r = run_bass_kernel_spmd(nc, [arrays], core_ids=[0])
    return np.ascontiguousarray(r.results[0]["out_0"].T)
```

```python
from contextlib import ExitStack

import concourse.bass as bass
from concourse import mybir

P = 128
N = 10000
HID = 128
NB = 20
BW = N // NB
CH = N // P
TAIL = N - CH * P
PIECES = 20
SIZES = [CH // PIECES + (r < CH % PIECES) for r in range(PIECES)]
STARTS = [sum(SIZES[:r]) for r in range(PIECES)]
MAXC = max(SIZES)
RAW = 4
CUT = 4
HALF = 2
HALVES = 2 * PIECES
LAST = PIECES - 1
assert PIECES % RAW == 0 and HALVES % CUT == 0 and SIZES[LAST] < MAXC == 2 * HALF
SUB = 4
SW = BW // SUB
QUADS = (CH + 1 + 3) // 4
EPS = 1e-5

K = 250
L = N // K
W = 48
STEPS = W + L
HANDOVER_TOL = 2.0 ** -19
GATES = (1, 0, 2, 3)

AT = dict(relu=1, x1=2, bias=2, centre2=3, copy2=5, var2=5, eps2=7, diag2=8, bcast2=9, norm2=11,
          centre1=12, copy1=14, var1=14, eps1=16, diag1=17, bcast1=18, norm1=19,
          store=9, load=11)


def program(nc, xT, itemT, adj_main, adj_tail, w_itemT, b_item, w_userT, b_user, w_ihT, w_hhT,
            b_ih, b_hh, w_linT, b_lin, fw, bw, out):
    f32 = mybir.dt.float32
    f32r = mybir.dt.float32r
    i32 = mybir.dt.int32
    ALU = mybir.AluOpType
    ACT = mybir.ActivationFunctionType
    ds = bass.ds

    x1_dram = nc.dram_tensor("x1_copy", (P, N), f32).ap()

    ctx = ExitStack()
    with ctx:
        def sb(name, shape, dt=f32, where=ctx):
            return where.enter_context(nc.sbuf_tensor(name, shape, dt))

        def pb(name, shape, where=ctx):
            return where.enter_context(nc.psum_tensor(name, shape, f32))

        def sem(name):
            return ctx.enter_context(nc.semaphore(name))

        u = sb("u", [P, W + N])
        centre = sb("centre", [P, P])
        ident = sb("ident", [P, P])
        ones = sb("ones", [P, P])
        mean_col = sb("mean_col", [P, 1])
        minus_half = sb("minus_half", [P, 1])
        inv_rows = sb("inv_rows", [2, P])
        wi = sb("wi", [P, HID])
        wu = sb("wu", [P, HID])
        bi = sb("bi", [P, HID])
        bu = sb("bu", [P, 1])
        wx = sb("wx", [P, 4 * HID])
        wh = sb("wh", [P, 4 * HID])
        wl = sb("wl", [P, 2])
        bl = sb("bl", [P, 2])
        wdc = sb("wdc", [P, 1])
        thr0 = sb("thr0", [P, 1])
        thr = sb("thr", [P, 1])
        fwc = sb("fwc", [P, 1])
        bwc = sb("bwc", [P, 1])
        hfw = sb("hfw", [P, 1])
        mbw = sb("mbw", [P, 1])
        okmin = sb("okmin", [P, 1])
        flag = sb("flag", [P, 1], i32)
        total = sb("total", [P, 1])

        first = ExitStack()
        item_hi = sb("item_hi", [P, (CH + 1) * HID], f32r, first)
        item_lo = sb("item_lo", [P, (CH + 1) * HID], f32r, first)
        raw = sb("raw", [P, RAW, MAXC * BW], f32, first)
        a_hi = sb("a_hi", [P, CUT, HALF * BW], f32r, first)
        a_lo = sb("a_lo", [P, CUT, HALF * BW], f32r, first)
        xb = sb("xb", [P, 2, BW], f32, first)
        v = sb("v", [P, BW], f32, first)
        xc = sb("xc", [P, BW], f32, first)
        sq = sb("sq", [P, BW], f32, first)
        un = sb("un", [P, BW], f32, first)
        rl = un
        diag = sb("diag", [SW, SUB, SW], f32, first)
        var = sb("var", [SW, SUB], f32, first)
        rstd = sb("rstd", [SW, SUB], f32, first)
        psG = pb("psG", [P, 2, 512], first)
        psN = pb("psN", [P, 512], first)
        psI = pb("psI", [P, 2, 512], first)
        psW = pb("psW", [P, 512], first)
        first.close()
        wx_raw = raw[:, RAW - 1, 0:4 * HID]
        bb = raw[0:2, RAW - 1, 4 * HID:8 * HID]

        x1 = sb("x1", [P, N])
        xh = sb("xh", [P, N])
        hist = sb("hist", [P, N])
        gt = sb("gt", [P, 4, K])
        fc = sb("fc", [P, K])
        ig = sb("ig", [P, K])
        C = sb("C", [P, K])
        H = sb("H", [P, K])
        th = sb("th", [P, K])
        H0 = sb("H0", [P, K])
        C0 = sb("C0", [P, K])
        dif = sb("dif", [P, 2 * (K - 1)])
        wd = sb("wd", [P, HID])
        w_g = sb("w_g", [P, 2, BW])
        pf = sb("pf", [P, 2, BW])
        sf = sb("sf", [P, 2, BW])
        psZ = pb("psZ", [P, 8, 512])
        inc = u

        w_in = sem("w_in")
        wx_in = sem("wx_in")
        x_in = [sem("x_in0"), sem("x_in1")]
        item_in = sem("item_in")
        raw_in = [sem(f"raw_in{s}") for s in range(RAW)]
        xb_in = sem("xb_in")
        hi_ready = sem("hi_ready")
        lo_ready = sem("lo_ready")
        halves_done = sem("halves_done")
        x1_stored = sem("x1_stored")
        const_ready = sem("const_ready")
        wx_psum = sem("wx_psum")
        prep = sem("prep")
        item_psum = sem("item_psum")
        item_sum = sem("item_sum")
        item_hi_ready = sem("item_hi_ready")
        item_ready = sem("item_ready")
        v_ready = sem("v_ready")
        relu_done = sem("relu_done")
        x1_ready = sem("x1_ready")
        ln_centred = sem("ln_centred")
        ln_squared = sem("ln_squared")
        ln_var = sem("ln_var")
        ln_eps = sem("ln_eps")
        ln_rstd = sem("ln_rstd")
        ln_diag = sem("ln_diag")
        ln_bcast = sem("ln_bcast")
        ln_out = sem("ln_out")
        u_ready = sem("u_ready")
        x1_back = sem("x1_back")
        zeroed = sem("zeroed")
        z_ready = sem("z_ready")
        t_ready = sem("t_ready")
        parts = sem("parts")
        c_ready = sem("c_ready")
        th_ready = sem("th_ready")
        h_ready = sem("h_ready")
        bound = sem("bound")
        hist_ready = sem("hist_ready")
        xh_ready = sem("xh_ready")
        check = sem("check")
        ok_sum = sem("ok_sum")
        flag_ready = sem("flag_ready")
        settled = sem("settled")
        g_z = sem("g_z")
        g_t = sem("g_t")
        g_parts = sem("g_parts")
        g_c = sem("g_c")
        g_th = sem("g_th")
        g_h = sem("g_h")
        g_hist = sem("g_hist")
        g_xh = sem("g_xh")
        d_ready = sem("d_ready")
        gated = sem("gated")
        summed = sem("summed")
        prefixed = sem("prefixed")
        added = sem("added")
        total_ready = sem("total_ready")
        suffixed = sem("suffixed")
        out_ready_v = sem("out_ready_v")
        out_ready_p = sem("out_ready_p")
        out_done = sem("out_done")

        def cols(c0, n=1):
            return slice(c0 * BW, (c0 + n) * BW)

        def half_cols(r, h):
            n = HALF if h == 0 else SIZES[r] - HALF + (r == LAST)
            return n * BW, h * HALF * BW

        def by_pool(f):
            return f // 2 % 3 == 2

        block = ctx.enter_context(nc.Block())

        @block.sync
        def _(sp):
            half = (CH // 2) * P
            sp.dma_start(u[:, W:W + half], itemT[:, 0:half]).then_inc(item_in, 16)
            sp.dma_start(u[:, W + half:W + N], itemT[:, half:N]).then_inc(item_in, 16)

            def load_block(j, wait=True, move=True, prefetch=True):
                for r in range(PIECES):
                    if wait or r >= RAW:
                        sp.wait_ge(lo_ready, HALVES * j + 2 * (r - RAW + 1))
                    elif r == RAW - 1:
                        sp.wait_ge(wx_psum, 1)
                    sp.dma_start(raw[:, r % RAW, 0:SIZES[r] * BW],
                                 adj_main[j, :, STARTS[r] * BW:(STARTS[r] + SIZES[r]) * BW])\
                        .then_inc(raw_in[r % RAW], 16)
                    if r == LAST:
                        sp.dma_start(raw[0:TAIL, r % RAW, SIZES[r] * BW:(SIZES[r] + 1) * BW], adj_tail[j])\
                            .then_inc(raw_in[r % RAW], 16)
                    if move and r == AT["store"]:
                        sp.wait_ge(x1_ready, j)
                        sp.dma_start(x1_dram[:, ds((j - 1) * BW, BW)], xb[:, (j + 1) % 2, :])\
                            .then_inc(x1_stored, 16)
                    if move and prefetch and r == AT["load"]:
                        sp.wait_ge(x1_stored, 16 * j)
                        sp.wait_ge(ln_centred, 2 * j + 1)
                        sp.dma_start(xb[:, (j + 1) % 2, :], xT[:, ds((j + 1) * BW, BW)]).then_inc(xb_in, 16)

            load_block(0, wait=False, move=False)
            with nc.sync.Fori(1, NB - 1) as j:
                load_block(j)
            load_block(NB - 1, prefetch=False)
            sp.wait_ge(x1_ready, NB)
            sp.wait_ge(x1_stored, 16 * (NB - 1))
            sp.dma_start(x1_dram[:, cols(NB - 1)], xb[:, (NB - 1) % 2, :]).then_inc(x1_stored, 16)
            sp.wait_ge(x1_stored, 16 * NB)
            sp.wait_ge(u_ready, NB)
            sp.dma_start(x1[:, :], x1_dram).then_inc(x1_back, 16)
            nv = np_ = 0
            for f in range(0, NB, 2):
                if by_pool(f):
                    np_ += 2
                    sp.wait_ge(out_ready_p, np_)
                else:
                    nv += 2
                    sp.wait_ge(out_ready_v, nv)
                sp.dma_start(out[:, cols(f, 2)], xh[:, cols(f, 2)]).then_inc(out_done, 16)
            sp.wait_ge(out_done, 16 * NB // 2)

        @block.gpsimd
        def _(pool):
            pool.memset(ident[:, :], 0.0).then_inc(const_ready, 1)
            pool.memset(centre[:, :], -1.0 / HID).then_inc(const_ready, 1)
            pool.memset(ones[:, :], 1.0).then_inc(const_ready, 1)
            pool.memset(mean_col[:, :], 1.0 / HID).then_inc(const_ready, 1)
            pool.memset(minus_half[:, :], -0.5).then_inc(const_ready, 1)
            pool.memset(inv_rows[:, :], 1.0 / HID).then_inc(const_ready, 1)
            pool.memset(u[:, 0:W], 0.0).then_inc(const_ready, 1)
            pool.wait_ge(const_ready, 7)
            for m, d in ((ident, 1.0), (centre, 1.0 - 1.0 / HID)):
                pool.affine_select(out=m[:, :], in_=m[:, :], compare_op=ALU.not_equal, fill=d,
                                   base=0, pattern=[[-1, P]], channel_multiplier=1)\
                    .then_inc(const_ready, 1)

            def inv_std(m):
                pool.wait_ge(ln_eps, m + 1)
                pool.tensor_tensor(rstd[:, :], var[:, :], minus_half[0:SW, :].to_broadcast([SW, SUB]),
                                   ALU.pow).then_inc(ln_rstd, 1)

            def plus_one(j):
                pool.wait_ge(ln_out, j + 1)
                pool.tensor_tensor(u[:, ds(W + j * BW, BW)], un[:, :],
                                   ones[:, 0:1].to_broadcast([P, BW]), ALU.add).then_inc(u_ready, 1)

            inv_std(0)
            inv_std(1)
            with nc.gpsimd.Fori(1, NB - 1) as j:
                inv_std(2 * j)
                plus_one(j - 1)
                inv_std(2 * j + 1)
            inv_std(2 * (NB - 1))
            plus_one(NB - 2)
            inv_std(2 * NB - 1)
            plus_one(NB - 1)

            pool.wait_ge(x1_back, 16)
            with nc.gpsimd.Fori(0, L) as s:
                pool.wait_ge(h_ready, W + 2 + s)
                pool.tensor_tensor(xh[:, ds(s, K, L)], x1[:, ds(s, K, L)], H[:, :], ALU.add)\
                    .then_inc(xh_ready, 1)

            pool.wait_ge(xh_ready, L)
            pool.wait_ge(flag_ready, 1)
            redo = pool.value_load(flag[0:1, 0:1], min_val=0, max_val=1)
            with pool.If(redo > 0):
                pool.wait_ge(g_hist, N)
                with nc.gpsimd.Fori(0, NB) as f:
                    pool.tensor_tensor(xh[:, ds(f * BW, BW)], x1[:, ds(f * BW, BW)], hist[:, ds(f * BW, BW)],
                                       ALU.add).then_inc(g_xh, 1)
                pool.wait_ge(g_xh, NB)
            for f in range(NB):
                pool.wait_ge(prefixed, f + 1)
                pool.tensor_tensor(xh[:, cols(f)], xh[:, cols(f)], pf[:, f % 2, :], ALU.add).then_inc(added, 1)
            for f in range(NB):
                if by_pool(f):
                    pool.wait_ge(suffixed, f + 1)
                    pool.wait_ge(added, f + 1)
                    pool.tensor_tensor(xh[:, cols(f)], xh[:, cols(f)], sf[:, f % 2, :], ALU.add)\
                        .then_inc(out_ready_p, 1)

        @block.scalar
        def _(act):
            act.dma_start(wi[:, :], w_itemT).then_inc(w_in, 16)
            act.dma_start(bi[:, :], b_item[0:1, :].to_broadcast([P, HID])).then_inc(w_in, 16)
            act.dma_start(xb[:, 0, :], xT[:, cols(0)]).then_inc(x_in[0], 16)
            act.dma_start(wx_raw, w_ihT).then_inc(wx_in, 16)
            act.dma_start(bb[0:1, :], b_ih).then_inc(wx_in, 16)
            act.dma_start(bb[1:2, :], b_hh).then_inc(wx_in, 16)
            act.dma_start(wu[:, :], w_userT).then_inc(w_in, 16)
            act.dma_start(bu[:, :], b_user).then_inc(w_in, 16)
            act.dma_start(wh[:, :], w_hhT).then_inc(w_in, 16)
            act.dma_start(wl[:, :], w_linT).then_inc(w_in, 16)
            act.dma_start(bl[:, :], b_lin[0:1, :].to_broadcast([P, 2])).then_inc(w_in, 16)
            act.dma_start(fwc[:, :], fw).then_inc(w_in, 16)
            act.dma_start(bwc[:, :], bw).then_inc(w_in, 16)
            act.dma_start(xb[:, 1, :], xT[:, cols(1)]).then_inc(x_in[1], 16)

            def relu(j):
                act.wait_ge(halves_done, HALVES * (j + 1))
                if isinstance(j, int) and j == NB - 1:
                    act.wait_ge(u_ready, j)
                else:
                    act.wait_ge(v_ready, j + 2)
                nc.scalar.activation(rl[:, :], psG[:, j % 2, 0:BW], ACT.Relu, bias=bu[:, 0:1])\
                    .then_inc(relu_done, 1)

            def copy_square(m, reader, count):
                act.wait_ge(ln_centred, m + 1)
                if reader is not None:
                    act.wait_ge(reader, count)
                nc.scalar.activation(xc[:, :], psN[:, 0:BW], ACT.Copy)
                nc.scalar.activation(sq[:, :], psN[:, 0:BW], ACT.Square).then_inc(ln_squared, 1)

            def split_hi(j, r, h, wait=True):
                s = 2 * r + h
                n, at = half_cols(r, h)
                per_block = PIECES // RAW + (r % RAW == LAST % RAW)
                arrived = 16 * (per_block * j + r // RAW + 1 + (r == LAST))
                if h == 0:
                    act.wait_ge(raw_in[r % RAW], arrived)
                if wait or s >= CUT:
                    act.wait_ge(halves_done, HALVES * j + (s - CUT + 1))
                nc.scalar.activation(a_hi[:, s % CUT, 0:n], raw[:, r % RAW, at:at + n], ACT.Copy)\
                    .then_inc(hi_ready, 1)

            def body(j, wait=True, has2=True, has1=True):
                for r in range(PIECES):
                    split_hi(j, r, 0, wait)
                    split_hi(j, r, 1, wait)
                    if has2 and r == AT["relu"]:
                        relu(j - 1)
                    if has2 and r == AT["copy2"]:
                        copy_square(2 * j, v_ready, j + 1)
                    if has1 and r == AT["copy1"]:
                        copy_square(2 * j + 1, ln_out if has2 else v_ready, j if has2 else 1)

            def item_hi_part(q):
                act.wait_ge(item_sum, q + 1)
                n = min(4, CH + 1 - 4 * q) * HID
                src = u[:, W + 4 * q * P:W + 4 * q * P + n] if q < QUADS - 1 else sq[:, 0:n]
                nc.scalar.activation(item_hi[:, 4 * q * HID:4 * q * HID + n], src, ACT.Copy)\
                    .then_inc(item_hi_ready, 1)

            copy_square(0, None, 0)
            for q in range(QUADS):
                item_hi_part(q)
            body(0, wait=False, has2=False)
            with nc.scalar.Fori(1, NB - 1) as j:
                body(j)
            body(NB - 1, has1=False)
            relu(NB - 1)
            copy_square(2 * NB - 1, ln_out, NB - 1)

            def lstm(n, par):
                for i, q in enumerate(GATES):
                    act.wait_ge(z_ready, 4 * n + i + 1)
                    nc.scalar.activation(gt[:, q, :], psZ[:, 4 * par + q, 0:K], ACT.Tanh).then_inc(t_ready, 1)
                act.wait_ge(c_ready, n + 1)
                nc.scalar.activation(th[:, :], C[:, :], ACT.Tanh, scale=0.5).then_inc(th_ready, 1)

            with nc.scalar.Fori(0, STEPS // 2) as i:
                lstm(2 * i, 0)
                lstm(2 * i + 1, 1)

            act.wait_ge(flag_ready, 1)
            redo = act.value_load(flag[0:1, 0:1], min_val=0, max_val=1)
            with act.If(redo > 0):
                with nc.scalar.Fori(0, N) as t:
                    act.wait_ge(g_z, t + 1)
                    nc.scalar.activation(gt[:, 0, 0:4], psZ[:, 0, 0:4], ACT.Tanh).then_inc(g_t, 1)
                    act.wait_ge(g_c, t + 1)
                    nc.scalar.activation(th[:, 0:1], C[:, 0:1], ACT.Tanh, scale=0.5).then_inc(g_th, 1)

            for f in range(NB):
                act.wait_ge(summed, f + 1)
                if f >= 2:
                    act.wait_ge(added, f - 1)
                nc.scalar.activation(pf[:, f % 2, :], inc[:, cols(f)], ACT.Copy, scale=hfw[:, 0:1])\
                    .then_inc(prefixed, 1)
            act.wait_ge(total_ready, 1)
            nv = np_ = 0
            used = []
            for f in range(NB):
                if f >= 2:
                    s, n = used[f - 2]
                    act.wait_ge(s, n)
                nc.scalar.activation(sf[:, f % 2, :], inc[:, f * BW + 1:(f + 1) * BW + 1], ACT.Identity,
                                     scale=mbw[:, 0:1], bias=total[:, 0:1]).then_inc(suffixed, 1)
                if by_pool(f):
                    np_ += 1
                    used.append((out_ready_p, np_))
                else:
                    nv += 1
                    used.append((out_ready_v, nv))

        @block.tensor
        def _(pe):
            def centre_rows(j, reader, count):
                if reader is not None:
                    pe.wait_ge(reader, count)
                pe.matmul(psN[:, 0:BW], centre[:, :], xb[:, j % 2, :], start=True, stop=True)\
                    .then_inc(ln_centred, 1)

            def variance(m):
                pe.wait_ge(ln_squared, m + 1)
                for s in range(SUB):
                    last = pe.matmul(psN[0:SW, s:s + 1], sq[:, s * SW:(s + 1) * SW], mean_col[:, :],
                                     start=True, stop=True)
                last.then_inc(ln_var, 1)

            def broadcast(m):
                pe.wait_ge(ln_diag, m + 1)
                pe.matmul(psN[:, 0:BW], ones[0:SW, :], diag[:, :, :].rearrange("p s w -> p (s w)"),
                          start=True, stop=True).then_inc(ln_bcast, 1)

            def body(j, has2=True, has1=True):
                bank = psG[:, j % 2, 0:BW]
                for r in range(PIECES):
                    for h in range(2):
                        s = 2 * r + h
                        pe.wait_ge(lo_ready, HALVES * j + s + 1)
                        for i in range(half_cols(r, h)[0] // BW):
                            c = STARTS[r] + h * HALF + i
                            rows = P if c < CH else TAIL
                            hi = a_hi[0:rows, s % CUT, i * BW:(i + 1) * BW]
                            lo = a_lo[0:rows, s % CUT, i * BW:(i + 1) * BW]
                            w_hi = item_hi[0:rows, c * HID:(c + 1) * HID]
                            w_lo = item_lo[0:rows, c * HID:(c + 1) * HID]
                            pe.matmul(bank, w_hi, hi, start=(c == 0), stop=False)
                            pe.matmul(bank, w_hi, lo, start=False, stop=False)
                            last = pe.matmul(bank, w_lo, hi, start=False, stop=(c == CH))
                        last.then_inc(halves_done, 1)
                    if r == AT["bias"]:
                        pe.wait_ge(v_ready, j + 1)
                        pe.matmul(bank, wu[:, :], v[:, :], start=False, stop=False)
                    if has2 and r == AT["centre2"]:
                        pe.wait_ge(x1_ready, j)
                        centre_rows(j - 1, v_ready, j + 1)
                    if has2 and r == AT["var2"]:
                        variance(2 * j)
                    if has2 and r == AT["bcast2"]:
                        broadcast(2 * j)
                    if has1 and r == AT["centre1"]:
                        if has2:
                            pe.wait_ge(xb_in, 16 * j)
                        else:
                            pe.wait_ge(x_in[1], 16)
                        centre_rows(j + 1, ln_out if has2 else v_ready, j if has2 else 1)
                    if has1 and r == AT["var1"]:
                        variance(2 * j + 1)
                    if has1 and r == AT["bcast1"]:
                        broadcast(2 * j + 1)

            pe.wait_ge(const_ready, 9)
            pe.wait_ge(x_in[0], 16)
            centre_rows(0, None, 0)
            pe.wait_ge(wx_in, 48)
            pe.matmul(psW[:, :], centre[:, :], wx_raw, start=True, stop=False)
            pe.matmul(psW[:, :], inv_rows[:, :], bb, start=False, stop=True).then_inc(wx_psum, 1)
            pe.wait_ge(w_in, 16 * 9)
            pe.wait_ge(item_in, 32)
            for q in range(QUADS):
                if q >= 2:
                    pe.wait_ge(item_sum, q - 1)
                for c in range(4 * q, min(4 * q + 4, CH + 1)):
                    rows = P if c < CH else TAIL
                    last = pe.matmul(psI[0:rows, q % 2, (c % 4) * HID:(c % 4 + 1) * HID],
                                     u[:, W + c * P:W + c * P + rows], wi[:, :], start=True, stop=True)
                last.then_inc(item_psum, 1)
                if q == 2:
                    variance(0)
                if q == 6:
                    broadcast(0)
            pe.wait_ge(item_ready, QUADS)

            body(0, has2=False)
            with nc.tensor.Fori(1, NB - 1) as j:
                body(j)
            body(NB - 1, has1=False)
            pe.wait_ge(x1_ready, NB)
            centre_rows(NB - 1, ln_out, NB - 1)
            variance(2 * NB - 1)
            broadcast(2 * NB - 1)

            def lstm(n, par, first_two=False):
                if not first_two:
                    pe.wait_ge(t_ready, 4 * n - 4)
                for q in GATES:
                    pe.matmul(psZ[:, 4 * par + q, 0:K], wx[:, q * HID:(q + 1) * HID], u[:, ds(n, K, L)],
                              start=True, stop=False)
                pe.wait_ge(h_ready, n + 1)
                for q in GATES:
                    pe.matmul(psZ[:, 4 * par + q, 0:K], wh[:, q * HID:(q + 1) * HID], H[:, :],
                              start=False, stop=True).then_inc(z_ready, 1)

            pe.wait_ge(prep, 12)
            pe.wait_ge(u_ready, NB)
            lstm(0, 0, first_two=True)
            lstm(1, 1, first_two=True)
            with nc.tensor.Fori(1, STEPS // 2) as i:
                lstm(2 * i, 0)
                lstm(2 * i + 1, 1)
            pe.wait_ge(check, 5)
            pe.wait_ge(th_ready, STEPS)
            pe.matmul(psZ[:, 0, 0:1], ones[:, :], okmin[:, :], start=True, stop=True).then_inc(ok_sum, 1)

            pe.wait_ge(flag_ready, 1)
            redo = pe.value_load(flag[0:1, 0:1], min_val=0, max_val=1)
            with pe.If(redo > 0):
                with nc.tensor.Fori(0, N) as t:
                    pe.wait_ge(g_h, t + 1)
                    for q in range(4):
                        pe.matmul(psZ[:, 0, q:q + 1], wx[:, q * HID:(q + 1) * HID], u[:, ds(W + t, 1)],
                                  start=True, stop=False)
                        last = pe.matmul(psZ[:, 0, q:q + 1], wh[:, q * HID:(q + 1) * HID], H[:, 0:1],
                                         start=False, stop=True)
                    last.then_inc(g_z, 1)
            pe.wait_ge(settled, 1)
            for f in range(NB):
                if f >= 2:
                    pe.wait_ge(gated, f - 1)
                pe.matmul(psZ[:, 2 + f % 2, 0:BW], wd[:, :], hist[:, cols(f)], start=True, stop=True)\
                    .then_inc(d_ready, 1)

        @block.vector
        def _(dve):
            def eps(m):
                dve.wait_ge(ln_var, m + 1)
                dve.tensor_scalar(var[:, :], psN[0:SW, 0:SUB], EPS, None, ALU.add).then_inc(ln_eps, 1)

            def diagonal(m):
                dve.wait_ge(ln_rstd, m + 1)
                dve.tensor_tensor(diag[:, :, :], ident[0:SW, 0:SW].unsqueeze(1).to_broadcast([SW, SUB, SW]),
                                  rstd[:, :].unsqueeze(2).to_broadcast([SW, SUB, SW]), ALU.mult)\
                    .then_inc(ln_diag, 1)

            def norm1(m):
                dve.wait_ge(ln_bcast, m + 1)
                dve.tensor_tensor(v[:, :], xc[:, :], psN[:, 0:BW], ALU.mult).then_inc(v_ready, 1)

            def norm2(m):
                dve.wait_ge(ln_bcast, m + 1)
                dve.tensor_tensor(un[:, :], xc[:, :], psN[:, 0:BW], ALU.mult).then_inc(ln_out, 1)

            def add_relu(j):
                dve.wait_ge(relu_done, j + 1)
                dve.tensor_tensor(xb[:, j % 2, :], xb[:, j % 2, :], rl[:, :], ALU.add).then_inc(x1_ready, 1)

            def split_lo(j, r, h):
                s = 2 * r + h
                n, at = half_cols(r, h)
                dve.wait_ge(hi_ready, HALVES * j + s + 1)
                dve.tensor_tensor(a_lo[:, s % CUT, 0:n], raw[:, r % RAW, at:at + n],
                                  a_hi[:, s % CUT, 0:n].bitcast(f32), ALU.subtract).then_inc(lo_ready, 1)

            def body(j, has2=True, has1=True):
                for r in range(PIECES):
                    split_lo(j, r, 0)
                    split_lo(j, r, 1)
                    if has2 and r == AT["x1"]:
                        add_relu(j - 1)
                    if has2 and r == AT["eps2"]:
                        eps(2 * j)
                    if has2 and r == AT["diag2"]:
                        diagonal(2 * j)
                    if has2 and r == AT["norm2"]:
                        norm2(2 * j)
                    if has1 and r == AT["eps1"]:
                        eps(2 * j + 1)
                    if has1 and r == AT["diag1"]:
                        diagonal(2 * j + 1)
                    if has1 and r == AT["norm1"]:
                        norm1(2 * j + 1)

            dve.wait_ge(wx_psum, 1)
            dve.tensor_scalar(wx[:, 0:2 * HID], psW[:, 0:2 * HID], 0.5, None, ALU.mult).then_inc(prep, 1)
            dve.tensor_scalar(wx[:, 2 * HID:3 * HID], psW[:, 2 * HID:3 * HID], 1.0, None, ALU.mult).then_inc(prep, 1)
            dve.tensor_scalar(wx[:, 3 * HID:4 * HID], psW[:, 3 * HID:4 * HID], 0.5, None, ALU.mult).then_inc(prep, 1)
            dve.wait_ge(w_in, 16 * 9)
            dve.wait_ge(const_ready, 9)
            for q in range(QUADS):
                n = min(4, CH + 1 - 4 * q)
                dve.wait_ge(item_psum, q + 1)
                if q < QUADS - 1:
                    dst = u[:, W + 4 * q * P:W + (4 * q + n) * P]
                    dve.tensor_tensor(dst.rearrange("p (c h) -> p c h", h=HID),
                                      psI[:, q % 2, 0:n * HID].rearrange("p (c h) -> p c h", h=HID),
                                      bi[:, :].unsqueeze(1).to_broadcast([P, n, HID]), ALU.add)\
                        .then_inc(item_sum, 1)
                    dve.wait_ge(item_hi_ready, q + 1)
                    dve.tensor_tensor(item_lo[:, 4 * q * HID:(4 * q + n) * HID], dst,
                                      item_hi[:, 4 * q * HID:(4 * q + n) * HID].bitcast(f32), ALU.subtract)\
                        .then_inc(item_ready, 1)
                if q == 2:
                    eps(0)
                if q == 4:
                    diagonal(0)
                if q == 6:
                    norm1(0)
            dve.memset(sq[:, 0:n * HID], 0.0).then_inc(prep, 1)
            dve.wait_ge(prep, 4)
            for c0, c1, rows in ((0, n - 1, P), (n - 1, n, TAIL)):
                dve.tensor_tensor(sq[0:rows, c0 * HID:c1 * HID].rearrange("p (c h) -> p c h", h=HID),
                                  psI[0:rows, (QUADS - 1) % 2, c0 * HID:c1 * HID].rearrange("p (c h) -> p c h", h=HID),
                                  bi[0:rows, :].unsqueeze(1).to_broadcast([rows, c1 - c0, HID]), ALU.add)\
                    .then_inc(item_sum if rows == TAIL else prep, 1)
            dve.wait_ge(prep, 5)
            dve.wait_ge(item_hi_ready, QUADS)
            dve.tensor_tensor(item_lo[:, 4 * q * HID:(4 * q + n) * HID], sq[:, 0:n * HID],
                              item_hi[:, 4 * q * HID:(4 * q + n) * HID].bitcast(f32), ALU.subtract)\
                .then_inc(item_ready, 1)

            body(0, has2=False)
            dve.tensor_scalar(wh[:, 0:2 * HID], wh[:, 0:2 * HID], 0.25, None, ALU.mult).then_inc(prep, 1)
            dve.tensor_scalar(wh[:, 2 * HID:3 * HID], wh[:, 2 * HID:3 * HID], 0.5, None, ALU.mult).then_inc(prep, 1)
            dve.tensor_scalar(wh[:, 3 * HID:4 * HID], wh[:, 3 * HID:4 * HID], 0.25, None, ALU.mult).then_inc(prep, 1)
            dve.tensor_tensor(wdc[:, :], wl[:, 1:2], wl[:, 0:1], ALU.subtract).then_inc(prep, 1)
            dve.tensor_tensor(thr0[:, :], bl[:, 0:1], bl[:, 1:2], ALU.subtract).then_inc(prep, 1)
            dve.tensor_scalar(hfw[:, :], fwc[:, :], 0.5, None, ALU.mult).then_inc(prep, 1)
            dve.tensor_scalar(mbw[:, :], bwc[:, :], -0.5, None, ALU.mult).then_inc(prep, 1)
            with nc.vector.Fori(1, NB - 1) as j:
                body(j)
            body(NB - 1, has1=False)
            add_relu(NB - 1)
            eps(2 * NB - 1)
            diagonal(2 * NB - 1)
            norm2(2 * NB - 1)

            dve.wait_ge(u_ready, NB)
            dve.memset(C[:, :], 0.0).then_inc(zeroed, 1)
            dve.memset(H[:, :], 0.0).then_inc(h_ready, 1)
            dve.wait_ge(prep, 12)
            dve.tensor_scalar(thr[:, :], thr0[:, :], 2.0, None, ALU.mult).then_inc(prep, 1)
            dve.tensor_scalar(wd[:, :], ones[:, :], wdc[:, 0:1], None, ALU.mult).then_inc(prep, 1)
            dve.wait_ge(zeroed, 1)
            dve.wait_ge(h_ready, 1)

            def lstm(n, kind):
                dve.wait_ge(t_ready, 4 * n + 1)
                dve.scalar_tensor_tensor(fc[:, :], gt[:, 1, :], 1.0, C[:, :], ALU.add, ALU.mult)\
                    .then_inc(parts, 1)
                dve.wait_ge(t_ready, 4 * n + 3)
                dve.scalar_tensor_tensor(ig[:, :], gt[:, 0, :], 1.0, gt[:, 2, :], ALU.add, ALU.mult)\
                    .then_inc(parts, 1)
                dve.wait_ge(parts, 2 * n + 2)
                dve.scalar_tensor_tensor(C[:, :], fc[:, :], 0.5, ig[:, :], ALU.mult, ALU.add)\
                    .then_inc(c_ready, 1)
                dve.wait_ge(t_ready, 4 * n + 4)
                dve.wait_ge(th_ready, n + 1)
                if kind == "main-again":
                    dve.wait_ge(xh_ready, n - W)
                h_step = dve.scalar_tensor_tensor(H[:, :], gt[:, 3, :], 1.0, th[:, :], ALU.add, ALU.mult)
                if kind == "boundary":
                    h_step.then_inc(bound, 1)
                    dve.wait_ge(bound, 1)
                    dve.memset(C[:, 0:1], 0.0).then_inc(zeroed, 1)
                    dve.memset(H[:, 0:1], 0.0).then_inc(h_ready, 1)
                    dve.wait_ge(zeroed, 2)
                    dve.wait_ge(h_ready, n + 2)
                    dve.tensor_copy(C0[:, :], C[:, :]).then_inc(zeroed, 1)
                    dve.tensor_copy(H0[:, :], H[:, :]).then_inc(zeroed, 1)
                else:
                    h_step.then_inc(h_ready, 1)
                if kind in ("main", "main-again"):
                    dve.wait_ge(h_ready, n + 2)
                    dve.tensor_copy(hist[:, ds(n - W, K, L)], H[:, :]).then_inc(hist_ready, 1)

            with nc.vector.Fori(0, W - 1) as n:
                lstm(n, "run-in")
            lstm(W - 1, "boundary")
            lstm(W, "main")
            with nc.vector.Fori(W + 1, STEPS) as n:
                lstm(n, "main-again")

            dve.wait_ge(h_ready, STEPS + 1)
            dve.wait_ge(c_ready, STEPS)
            dve.wait_ge(zeroed, 4)
            dve.tensor_tensor(dif[:, 0:K - 1], H[:, 0:K - 1], H0[:, 1:K], ALU.subtract).then_inc(check, 1)
            dve.tensor_tensor(dif[:, K - 1:], C[:, 0:K - 1], C0[:, 1:K], ALU.subtract).then_inc(check, 1)
            dve.wait_ge(check, 2)
            dve.tensor_tensor(dif[:, :], dif[:, :], dif[:, :], ALU.mult).then_inc(check, 1)
            dve.wait_ge(check, 3)
            dve.tensor_scalar(dif[:, :], dif[:, :], HANDOVER_TOL ** 2, None, ALU.is_le).then_inc(check, 1)
            dve.wait_ge(check, 4)
            dve.tensor_reduce(okmin[:, :], dif[:, :], mybir.AxisListType.X, ALU.min).then_inc(check, 1)
            dve.wait_ge(ok_sum, 1)
            dve.tensor_scalar(flag[:, :], psZ[:, 0, 0:1], float(P) - 0.5, None, ALU.is_lt).then_inc(flag_ready, 1)
            dve.wait_ge(flag_ready, 1)
            redo = dve.value_load(flag[0:1, 0:1], min_val=0, max_val=1)
            with dve.If(redo > 0):
                dve.wait_ge(xh_ready, L)
                dve.wait_ge(hist_ready, L)
                dve.memset(C[:, 0:1], 0.0).then_inc(zeroed, 1)
                dve.wait_ge(zeroed, 5)
                dve.memset(H[:, 0:1], 0.0).then_inc(g_h, 1)
                with nc.vector.Fori(0, N) as t:
                    dve.wait_ge(g_t, t + 1)
                    dve.scalar_tensor_tensor(fc[:, 0:1], gt[:, 0, 1:2], 1.0, C[:, 0:1], ALU.add, ALU.mult)\
                        .then_inc(g_parts, 1)
                    dve.scalar_tensor_tensor(ig[:, 0:1], gt[:, 0, 0:1], 1.0, gt[:, 0, 2:3], ALU.add, ALU.mult)\
                        .then_inc(g_parts, 1)
                    dve.wait_ge(g_parts, 2 * t + 2)
                    dve.scalar_tensor_tensor(C[:, 0:1], fc[:, 0:1], 0.5, ig[:, 0:1], ALU.mult, ALU.add)\
                        .then_inc(g_c, 1)
                    dve.wait_ge(g_th, t + 1)
                    dve.scalar_tensor_tensor(H[:, 0:1], gt[:, 0, 3:4], 1.0, th[:, 0:1], ALU.add, ALU.mult)\
                        .then_inc(g_h, 1)
                    dve.wait_ge(g_h, t + 2)
                    dve.tensor_copy(hist[:, ds(t, 1)], H[:, 0:1]).then_inc(g_hist, 1)
                dve.wait_ge(g_hist, N)
            dve.wait_ge(hist_ready, L)
            dve.wait_ge(prep, 14)
            dve.memset(inc[:, 0:1], 0.0).then_inc(settled, 1)
            dve.wait_ge(settled, 1)

            for f in range(NB):
                dve.wait_ge(d_ready, f + 1)
                if f >= 2:
                    dve.wait_ge(summed, f - 1)
                dve.scalar_tensor_tensor(w_g[:, f % 2, :], psZ[:, 2 + f % 2, 0:BW], thr[:, 0:1], hist[:, cols(f)],
                                         ALU.is_gt, ALU.mult).then_inc(gated, 1)
                dve.wait_ge(gated, f + 1)
                if f:
                    dve.wait_ge(summed, f)
                dve.tensor_tensor_scan(inc[:, f * BW + 1:(f + 1) * BW + 1], w_g[:, f % 2, :], w_g[:, f % 2, :],
                                       inc[:, f * BW:f * BW + 1], ALU.add, ALU.bypass).then_inc(summed, 1)
            dve.wait_ge(summed, NB)
            dve.scalar_tensor_tensor(total[:, :], inc[:, N:N + 1], -1.0, mbw[:, :], ALU.mult, ALU.mult)\
                .then_inc(total_ready, 1)
            for f in range(NB):
                if not by_pool(f):
                    dve.wait_ge(added, f + 1)
                    dve.wait_ge(suffixed, f + 1)
                    dve.tensor_tensor(xh[:, cols(f)], xh[:, cols(f)], sf[:, f % 2, :], ALU.add)\
                        .then_inc(out_ready_v, 1)


def kernel(x, adj, L0_gnn_item_feat, L0_gnn_W_item, L0_gnn_b_item, L0_gnn_W_user, L0_gnn_b_user,
           L0_ffn_W_ih, L0_ffn_W_hh, L0_ffn_b_ih, L0_ffn_b_hh, L0_ffn_W_lin, L0_ffn_b_lin,
           L0_ffn_fw_att, L0_ffn_bw_att):
    import numpy as np
    import concourse.bacc as bacc
    from concourse.bass_utils import run_bass_kernel_spmd

    adjT = np.asarray(adj).T
    main = adjT[:CH * P].reshape(CH, P, NB, BW).transpose(2, 1, 0, 3).reshape(NB, P, CH * BW)
    short = adjT[CH * P:].reshape(TAIL, NB, BW).transpose(1, 0, 2)
    host = [
        ("xT", np.asarray(x).T), ("itemT", np.asarray(L0_gnn_item_feat).T),
        ("adj_main", main), ("adj_tail", short),
        ("w_itemT", np.asarray(L0_gnn_W_item).T), ("b_item", np.asarray(L0_gnn_b_item).reshape(1, HID)),
        ("w_userT", np.asarray(L0_gnn_W_user).T), ("b_user", np.asarray(L0_gnn_b_user).reshape(HID, 1)),
        ("w_ihT", np.asarray(L0_ffn_W_ih).T), ("w_hhT", np.asarray(L0_ffn_W_hh).T),
        ("b_ih", np.asarray(L0_ffn_b_ih).reshape(1, 4 * HID)), ("b_hh", np.asarray(L0_ffn_b_hh).reshape(1, 4 * HID)),
        ("w_linT", np.asarray(L0_ffn_W_lin).T), ("b_lin", np.asarray(L0_ffn_b_lin).reshape(1, 2)),
        ("fw", np.asarray(L0_ffn_fw_att).reshape(HID, 1)), ("bw", np.asarray(L0_ffn_bw_att).reshape(HID, 1)),
    ]
    nc = bacc.Bacc("TRN2", target_bir_lowering=False, num_devices=1)
    arrays, args = {}, []
    for name, a in host:
        a = np.ascontiguousarray(a)
        arrays[f"in_{name}"] = a
        args.append(nc.dram_tensor(f"in_{name}", a.shape, mybir.dt.from_np(a.dtype), kind="ExternalInput").ap())
    out = nc.dram_tensor("out_0", (HID, N), mybir.dt.float32, kind="ExternalOutput").ap()
    program(nc, *args, out)
    r = run_bass_kernel_spmd(nc, [arrays], core_ids=[0])
    return np.ascontiguousarray(r.results[0]["out_0"].T)
```

```python
from contextlib import ExitStack

import concourse.bass as bass
from concourse import mybir

P = 128
N = 10000
HID = 128
NB = 20
BW = N // NB
CH = N // P
TAIL = N - CH * P
PIECES = 20
SIZES = [CH // PIECES + (r < CH % PIECES) for r in range(PIECES)]
STARTS = [sum(SIZES[:r]) for r in range(PIECES)]
MAXC = max(SIZES)
RAW = 4
CUT = 4
HALF = 2
HALVES = 2 * PIECES
LAST = PIECES - 1
assert PIECES % RAW == 0 and HALVES % CUT == 0 and SIZES[LAST] < MAXC == 2 * HALF
SUB = 4
SW = BW // SUB
QUADS = (CH + 1 + 3) // 4
AHEAD = 3
PARTS = (0, 1, 4, 8, 12, 16, QUADS)
EPS = 1e-5

K = 250
L = N // K
W = 48
STEPS = W + L
KH = K // 2
XC = 256
assert K % 2 == 0 and XC - K <= W
OUTS = 25
OW = N // OUTS
HANDOVER_TOL = 2.0 ** -19
assert OW % L == 0 and W % 2 == 0 and L % 2 == 0
CELL = 2
GATES = (1, 0, 2, 3)

AT = dict(relu=1, x1=2, bias=2, centre2=3, copy2=5, var2=5, eps2=7, diag2=8, bcast2=9, norm2=11,
          centre1=12, copy1=14, var1=14, eps1=16, diag1=17, bcast1=18, norm1=19,
          store=9, load=11, wx=10)


def program(nc, xT, itemT, adj_main, adj_tail, w_itemT, b_item, w_userT, b_user, w_ihT, w_hhT,
            b_ih, b_hh, w_linT, b_lin, fw, bw, out):
    f32 = mybir.dt.float32
    f32r = mybir.dt.float32r
    i32 = mybir.dt.int32
    ALU = mybir.AluOpType
    ACT = mybir.ActivationFunctionType
    ds = bass.ds

    x1_dram = nc.dram_tensor("x1_copy", (P, N), f32).ap()

    ctx = ExitStack()
    with ctx:
        def sb(name, shape, dt=f32, where=ctx):
            return where.enter_context(nc.sbuf_tensor(name, shape, dt))

        def pb(name, shape, where=ctx):
            return where.enter_context(nc.psum_tensor(name, shape, f32))

        def sem(name):
            return ctx.enter_context(nc.semaphore(name))

        u = sb("u", [P, W + N])
        centre = sb("centre", [P, P])
        ident = sb("ident", [P, P])
        ones = sb("ones", [P, P])
        mean_col = sb("mean_col", [P, 1])
        minus_half = sb("minus_half", [P, 1])
        inv_rows = sb("inv_rows", [2, P])
        wi = sb("wi", [P, HID])
        wu = sb("wu", [P, HID])
        bi = sb("bi", [P, HID])
        bu = sb("bu", [P, 1])
        wx = sb("wx", [P, 4 * HID])
        wx_hi = sb("wx_hi", [P, 4 * HID], f32r)
        wx_lo = sb("wx_lo", [P, 4 * HID], f32r)
        wh = sb("wh", [P, 4 * HID])
        wl = sb("wl", [P, 2])
        bl = sb("bl", [P, 2])
        wdc = sb("wdc", [P, 1])
        thr0 = sb("thr0", [P, 1])
        thr = sb("thr", [P, 1])
        fwc = sb("fwc", [P, 1])
        bwc = sb("bwc", [P, 1])
        hfw = sb("hfw", [P, 1])
        dfb = sb("dfb", [P, 1])
        mbw = sb("mbw", [P, 1])
        okmin = sb("okmin", [P, 1])
        flag = sb("flag", [P, 1], i32)
        total = sb("total", [P, 1])

        first = ExitStack()
        item_hi = sb("item_hi", [P, (CH + 1) * HID], f32r, first)
        item_lo = sb("item_lo", [P, (CH + 1) * HID], f32r, first)
        raw = sb("raw", [P, RAW, MAXC * BW], f32, first)
        a_hi = sb("a_hi", [P, CUT, HALF * BW], f32r, first)
        a_lo = sb("a_lo", [P, CUT, HALF * BW], f32r, first)
        xb = sb("xb", [P, 2, BW], f32, first)
        v = sb("v", [P, BW], f32, first)
        xc = sb("xc", [P, BW], f32, first)
        sq = sb("sq", [P, BW], f32, first)
        un_bb = sb("un_bb", [P, 4 * HID], f32, first)
        bb = un_bb[0:2, :]
        un = un_bb[:, 0:BW]
        rl = un
        diag = sb("diag", [SW, SUB, SW], f32, first)
        var = sb("var", [SW, SUB], f32, first)
        rstd = sb("rstd", [SW, SUB], f32, first)
        psG = pb("psG", [P, 2, 512], first)
        psN = pb("psN", [P, 512], first)
        psI = pb("psI", [P, 2, 512], first)
        psW = pb("psW", [P, 512], first)
        first.close()


        x1 = sb("x1", [P, N])
        y = sb("y", [P, N])
        u_hi = sb("u_hi", [P, 2, XC], f32r)
        u_lo = sb("u_lo", [P, 2, XC], f32r)
        gt = sb("gt", [P, 4, K])
        fc = sb("fc", [P, K])
        ig = sb("ig", [P, K])
        C = sb("C", [P, K])
        H = sb("H", [P, 2, K])
        th = sb("th", [P, K])
        H0 = sb("H0", [P, K])
        C0 = sb("C0", [P, K])
        dif = sb("dif", [P, 2 * (K - 1)])
        wd = sb("wd", [P, HID])
        gh = sb("gh", [P, 2, K])
        run = sb("run", [P, 2, K])
        run_c = sb("run_c", [P, K])
        own = sb("own", [P, K])
        both = sb("both", [P, K])
        cum = sb("cum", [P, K + 1])
        shift = sb("shift", [P, K])
        g_gh = sb("g_gh", [P, BW])
        g_cum = sb("g_cum", [P, BW + 1])
        psZ = pb("psZ", [P, 8, 512])

        wi_in = sem("wi_in")
        w_in = sem("w_in")
        wx_in = sem("wx_in")
        x_in = [sem("x_in0"), sem("x_in1")]
        item_in = [sem(f"item_in{i}") for i in range(len(PARTS) - 1)]
        raw_in = [sem(f"raw_in{s}") for s in range(RAW)]
        xb_in = sem("xb_in")
        hi_ready = sem("hi_ready")
        lo_ready = sem("lo_ready")
        halves_done = sem("halves_done")
        x1_stored = sem("x1_stored")
        const_ready = sem("const_ready")
        wx_psum = sem("wx_psum")
        prep = sem("prep")
        dfb_ready = sem("dfb_ready")
        wd_ready = sem("wd_ready")
        item_psum = sem("item_psum")
        item_sum = sem("item_sum")
        item_hi_ready = sem("item_hi_ready")
        item_ready = sem("item_ready")
        v_ready = sem("v_ready")
        relu_done = sem("relu_done")
        x1_ready = sem("x1_ready")
        ln_centred = sem("ln_centred")
        ln_squared = sem("ln_squared")
        ln_var = sem("ln_var")
        ln_eps = sem("ln_eps")
        ln_rstd = sem("ln_rstd")
        ln_diag = sem("ln_diag")
        ln_bcast = sem("ln_bcast")
        ln_out = sem("ln_out")
        u_ready = sem("u_ready")
        x1_back = sem("x1_back")
        zeroed = sem("zeroed")
        u_hi_ready = sem("u_hi_ready")
        first_lo_ready = sem("first_lo_ready")
        u_lo_ready = sem("u_lo_ready")
        z_ready = sem("z_ready")
        t_ready = sem("t_ready")
        parts = sem("parts")
        c_ready = sem("c_ready")
        th_ready = sem("th_ready")
        h_ready = sem("h_ready")
        bound = sem("bound")
        d_ready = sem("d_ready")
        gated = sem("gated")
        own_ready = sem("own_ready")
        run_ready = sem("run_ready")
        run_c_ready = sem("run_c_ready")
        both_ready = sem("both_ready")
        y_ready = sem("y_ready")
        check = sem("check")
        ok_sum = sem("ok_sum")
        flag_ready = sem("flag_ready")
        cum_ready = sem("cum_ready")
        g_z = sem("g_z")
        g_t = sem("g_t")
        g_parts = sem("g_parts")
        g_c = sem("g_c")
        g_th = sem("g_th")
        g_h = sem("g_h")
        g_hist = sem("g_hist")
        g_d = sem("g_d")
        g_out = sem("g_out")
        g_terms = sem("g_terms")
        g_end = sem("g_end")
        total_ready = sem("total_ready")
        shift_ready = sem("shift_ready")
        out_ready_v = sem("out_ready_v")
        out_ready_p = sem("out_ready_p")
        out_done = sem("out_done")

        def cols(c0, n=1):
            return slice(c0 * BW, (c0 + n) * BW)

        def half_cols(r, h):
            n = HALF if h == 0 else SIZES[r] - HALF + (r == LAST)
            return n * BW, h * HALF * BW

        def by_pool(f):
            return f % 3 == 2

        def chunks_of(t, f):
            return t[:, f * OW:(f + 1) * OW].rearrange("p (k l) -> p k l", l=L)

        def shift_of(f):
            k = OW // L
            return shift[:, f * k:(f + 1) * k].unsqueeze(2).to_broadcast([P, k, L])

        block = ctx.enter_context(nc.Block())

        @block.sync
        def _(sp):
            def load_items(i):
                c0, c1 = 4 * PARTS[i] * P, min(4 * PARTS[i + 1] * P, N)
                sp.dma_start(u[:, W + c0:W + c1], itemT[:, c0:c1]).then_inc(item_in[i], 16)

            load_items(0)
            load_items(1)

            def load_block(j, wait=True, move=True, prefetch=True, items={}):
                for r in range(PIECES):
                    if wait or r >= RAW:
                        sp.wait_ge(lo_ready, HALVES * j + 2 * (r - RAW + 1))
                    sp.dma_start(raw[:, r % RAW, 0:SIZES[r] * BW],
                                 adj_main[j, :, STARTS[r] * BW:(STARTS[r] + SIZES[r]) * BW])\
                        .then_inc(raw_in[r % RAW], 16)
                    if r == LAST:
                        sp.dma_start(raw[0:TAIL, r % RAW, SIZES[r] * BW:(SIZES[r] + 1) * BW], adj_tail[j])\
                            .then_inc(raw_in[r % RAW], 16)
                    for i in items.get(r, ()):
                        load_items(i)
                    if move and r == AT["store"]:
                        sp.wait_ge(x1_ready, j)
                        sp.dma_start(x1_dram[:, ds((j - 1) * BW, BW)], xb[:, (j + 1) % 2, :])\
                            .then_inc(x1_stored, 16)
                    if move and prefetch and r == AT["load"]:
                        sp.wait_ge(x1_stored, 16 * j)
                        sp.wait_ge(ln_centred, 2 * j + 1)
                        sp.dma_start(xb[:, (j + 1) % 2, :], xT[:, ds((j + 1) * BW, BW)]).then_inc(xb_in, 16)

            load_block(0, wait=False, move=False, items={0: (2,), 2: (3,), 3: (4, 5)})
            with nc.sync.Fori(1, NB - 1) as j:
                load_block(j)
            load_block(NB - 1, prefetch=False)
            sp.wait_ge(x1_ready, NB)
            sp.wait_ge(x1_stored, 16 * (NB - 1))
            sp.dma_start(x1_dram[:, cols(NB - 1)], xb[:, (NB - 1) % 2, :]).then_inc(x1_stored, 16)
            sp.wait_ge(x1_stored, 16 * NB)
            sp.wait_ge(u_ready, NB)
            sp.dma_start(x1[:, :], x1_dram).then_inc(x1_back, 16)
            by_v = by_p = 0
            for f in range(OUTS):
                if by_pool(f):
                    by_p += 1
                    sp.wait_ge(out_ready_p, by_p)
                else:
                    by_v += 1
                    sp.wait_ge(out_ready_v, by_v)
                sp.dma_start(out[:, f * OW:(f + 1) * OW], y[:, f * OW:(f + 1) * OW]).then_inc(out_done, 16)
            sp.wait_ge(out_done, 16 * OUTS)

        @block.gpsimd
        def _(pool):
            pool.memset(ident[:, :], 0.0).then_inc(const_ready, 1)
            pool.memset(centre[:, :], -1.0 / HID).then_inc(const_ready, 1)
            pool.memset(ones[:, :], 1.0).then_inc(const_ready, 1)
            pool.memset(mean_col[:, :], 1.0 / HID).then_inc(const_ready, 1)
            pool.memset(minus_half[:, :], -0.5).then_inc(const_ready, 1)
            pool.memset(inv_rows[:, :], 1.0 / HID).then_inc(const_ready, 1)
            pool.memset(u[:, 0:W], 0.0).then_inc(const_ready, 1)
            pool.wait_ge(const_ready, 7)
            for m, d in ((ident, 1.0), (centre, 1.0 - 1.0 / HID)):
                pool.affine_select(out=m[:, :], in_=m[:, :], compare_op=ALU.not_equal, fill=d,
                                   base=0, pattern=[[-1, P]], channel_multiplier=1)\
                    .then_inc(const_ready, 1)

            def inv_std(m):
                pool.wait_ge(ln_eps, m + 1)
                pool.tensor_tensor(rstd[:, :], var[:, :], minus_half[0:SW, :].to_broadcast([SW, SUB]),
                                   ALU.pow).then_inc(ln_rstd, 1)

            def plus_one(j):
                pool.wait_ge(ln_out, j + 1)
                pool.tensor_tensor(u[:, ds(W + j * BW, BW)], un[:, :],
                                   ones[:, 0:1].to_broadcast([P, BW]), ALU.add).then_inc(u_ready, 1)

            inv_std(0)
            inv_std(1)
            with nc.gpsimd.Fori(1, NB - 1) as j:
                inv_std(2 * j)
                plus_one(j - 1)
                inv_std(2 * j + 1)
            inv_std(2 * (NB - 1))
            plus_one(NB - 2)
            inv_std(2 * NB - 1)
            plus_one(NB - 1)

            def chunk_sum(s, par, first=False):
                pool.wait_ge(gated, s + 1)
                if not first:
                    pool.wait_ge(run_ready, s + 1)
                    pool.wait_ge(run_c_ready, s)
                pool.tensor_tensor(run[:, 1 - par, :], run[:, par, :], gh[:, par, :], ALU.add)\
                    .then_inc(run_ready, 1)
                pool.wait_ge(run_c_ready, s + 1)
                pool.wait_ge(own_ready, s + 1)
                if not first:
                    pool.wait_ge(y_ready, s)
                pool.tensor_tensor(both[:, :], own[:, :], run_c[:, :], ALU.add).then_inc(both_ready, 1)
                pool.wait_ge(both_ready, s + 1)
                pool.tensor_tensor(y[:, ds(s, K, L)], x1[:, ds(s, K, L)], both[:, :], ALU.add)\
                    .then_inc(y_ready, 1)

            def input_lo(m, par):
                pool.wait_ge(u_hi_ready, m + 1)
                pool.tensor_tensor(u_lo[:, par, 0:K], u[:, ds(m, K, L)], u_hi[:, par, 0:K].bitcast(f32),
                                   ALU.subtract).then_inc(u_lo_ready, 1)

            with nc.gpsimd.Fori(0, W // 2) as i:
                input_lo(2 * i + 2, 0)
                input_lo(2 * i + 3, 1)
            pool.memset(run[:, 0, :], 0.0).then_inc(run_ready, 1)
            pool.wait_ge(x1_back, 16)
            pool.wait_ge(run_ready, 1)
            input_lo(W + 2, 0)
            input_lo(W + 3, 1)
            chunk_sum(0, 0, first=True)
            with nc.gpsimd.Fori(1, L // 2 - 1) as i:
                input_lo(W + 2 * i + 2, 0)
                chunk_sum(2 * i - 1, 1)
                input_lo(W + 2 * i + 3, 1)
                chunk_sum(2 * i, 0)
            for s in range(L - 3, L):
                chunk_sum(s, s % 2)

            pool.wait_ge(y_ready, L)
            pool.wait_ge(shift_ready, 1)
            for f in range(OUTS):
                if by_pool(f):
                    pool.tensor_tensor(chunks_of(y, f), chunks_of(y, f), shift_of(f), ALU.add)\
                        .then_inc(out_ready_p, 1)

        @block.scalar
        def _(act):
            act.dma_start(wi[:, :], w_itemT).then_inc(wi_in, 16)
            act.dma_start(bi[:, :], b_item[0:1, :].to_broadcast([P, HID])).then_inc(wi_in, 16)
            act.dma_start(xb[:, 0, :], xT[:, cols(0)]).then_inc(x_in[0], 16)
            act.dma_start(wx[:, :], w_ihT).then_inc(wx_in, 16)
            act.dma_start(bb[0:1, :], b_ih).then_inc(wx_in, 16)
            act.dma_start(bb[1:2, :], b_hh).then_inc(wx_in, 16)
            act.dma_start(wu[:, :], w_userT).then_inc(w_in, 16)
            act.dma_start(bu[:, :], b_user).then_inc(w_in, 16)
            act.dma_start(wh[:, :], w_hhT).then_inc(w_in, 16)
            act.dma_start(wl[:, :], w_linT).then_inc(w_in, 16)
            act.dma_start(bl[:, :], b_lin[0:1, :].to_broadcast([P, 2])).then_inc(w_in, 16)
            act.dma_start(fwc[:, :], fw).then_inc(w_in, 16)
            act.dma_start(bwc[:, :], bw).then_inc(w_in, 16)
            act.dma_start(xb[:, 1, :], xT[:, cols(1)]).then_inc(x_in[1], 16)

            def relu(j):
                act.wait_ge(halves_done, HALVES * (j + 1))
                if isinstance(j, int) and j == NB - 1:
                    act.wait_ge(u_ready, j)
                else:
                    act.wait_ge(v_ready, j + 2)
                nc.scalar.activation(rl[:, :], psG[:, j % 2, 0:BW], ACT.Relu, bias=bu[:, 0:1])\
                    .then_inc(relu_done, 1)

            def copy_square(m, reader, count):
                act.wait_ge(ln_centred, m + 1)
                if reader is not None:
                    act.wait_ge(reader, count)
                nc.scalar.activation(xc[:, :], psN[:, 0:BW], ACT.Copy)
                nc.scalar.activation(sq[:, :], psN[:, 0:BW], ACT.Square).then_inc(ln_squared, 1)

            def split_hi(j, r, h, wait=True):
                s = 2 * r + h
                n, at = half_cols(r, h)
                per_block = PIECES // RAW + (r % RAW == LAST % RAW)
                arrived = 16 * (per_block * j + r // RAW + 1 + (r == LAST))
                if h == 0:
                    act.wait_ge(raw_in[r % RAW], arrived)
                if wait or s >= CUT:
                    act.wait_ge(halves_done, HALVES * j + (s - CUT + 1))
                nc.scalar.activation(a_hi[:, s % CUT, 0:n], raw[:, r % RAW, at:at + n], ACT.Copy)\
                    .then_inc(hi_ready, 1)

            def body(j, wait=True, has2=True, has1=True, items=False):
                for r in range(PIECES):
                    split_hi(j, r, 0, wait)
                    split_hi(j, r, 1, wait)
                    if items and r + 1 < QUADS:
                        item_hi_part(r + 1)
                    if has2 and r == AT["relu"]:
                        relu(j - 1)
                    if has2 and r == AT["copy2"]:
                        copy_square(2 * j, v_ready, j + 1)
                    if has1 and r == AT["copy1"]:
                        copy_square(2 * j + 1, ln_out if has2 else v_ready, j if has2 else 1)

            def item_hi_part(q):
                act.wait_ge(item_sum, q + 1)
                n = min(4, CH + 1 - 4 * q) * HID
                src = u[:, W + 4 * q * P:W + 4 * q * P + n] if q < QUADS - 1 else sq[:, 0:n]
                nc.scalar.activation(item_hi[:, 4 * q * HID:4 * q * HID + n], src, ACT.Copy)\
                    .then_inc(item_hi_ready, 1)

            item_hi_part(0)
            copy_square(0, None, 0)
            body(0, wait=False, has2=False, items=True)
            with nc.scalar.Fori(1, NB - 1) as j:
                body(j)
            body(NB - 1, has1=False)
            relu(NB - 1)
            copy_square(2 * NB - 1, ln_out, NB - 1)

            def input_hi(m, par):
                nc.scalar.activation(u_hi[:, par, 0:K], u[:, ds(m, K, L)], ACT.Copy).then_inc(u_hi_ready, 1)

            def lstm(n, par, prefetch=True):
                for i, q in enumerate(GATES):
                    act.wait_ge(z_ready, 4 * n + i + 1)
                    halves = ((0, K),) if q != CELL else ((0, KH), (KH, K))
                    for a, b in halves:
                        nc.scalar.activation(gt[:, q, a:b], psZ[:, 4 * par + q, a:b], ACT.Tanh).then_inc(t_ready, 1)
                if prefetch:
                    input_hi(n + 2, par)
                act.wait_ge(c_ready, 2 * n + 1)
                nc.scalar.activation(th[:, 0:KH], C[:, 0:KH], ACT.Tanh, scale=0.5).then_inc(th_ready, 1)
                act.wait_ge(c_ready, 2 * n + 2)
                nc.scalar.activation(th[:, KH:K], C[:, KH:K], ACT.Tanh, scale=0.5).then_inc(th_ready, 1)

            def scale_run(s, par):
                act.wait_ge(run_ready, s + 1)
                if not (isinstance(s, int) and s == 0):
                    act.wait_ge(both_ready, s)
                nc.scalar.activation(run_c[:, :], run[:, par, :], ACT.Copy, scale=dfb[:, 0:1])\
                    .then_inc(run_c_ready, 1)

            act.wait_ge(u_ready, NB)
            nc.scalar.activation(u_hi[:, :, K:XC], u[:, 0:XC - K].unsqueeze(1).to_broadcast([P, 2, XC - K]), ACT.Copy)
            input_hi(0, 0)
            input_hi(1, 1)
            with nc.scalar.Fori(0, W // 2) as i:
                lstm(2 * i, 0)
                lstm(2 * i + 1, 1)
            lstm(W, 0)
            lstm(W + 1, 1)
            act.wait_ge(dfb_ready, 1)
            scale_run(0, 0)
            with nc.scalar.Fori(1, L // 2 - 1) as i:
                lstm(W + 2 * i, 0)
                scale_run(2 * i - 1, 1)
                lstm(W + 2 * i + 1, 1)
                scale_run(2 * i, 0)
            lstm(STEPS - 2, 0, prefetch=False)
            scale_run(L - 3, 1)
            lstm(STEPS - 1, 1, prefetch=False)
            scale_run(L - 2, 0)
            scale_run(L - 1, 1)

            act.wait_ge(flag_ready, 1)
            redo = act.value_load(flag[0:1, 0:1], min_val=0, max_val=1)
            with act.If(redo > 0):
                with nc.scalar.Fori(0, N) as t:
                    act.wait_ge(g_z, t + 1)
                    nc.scalar.activation(gt[:, 0, 0:4], psZ[:, 0, 0:4], ACT.Tanh).then_inc(g_t, 1)
                    act.wait_ge(g_c, t + 1)
                    nc.scalar.activation(th[:, 0:1], C[:, 0:1], ACT.Tanh, scale=0.5).then_inc(g_th, 1)

        @block.tensor
        def _(pe):
            def centre_rows(j, reader, count):
                if reader is not None:
                    pe.wait_ge(reader, count)
                pe.matmul(psN[:, 0:BW], centre[:, :], xb[:, j % 2, :], start=True, stop=True)\
                    .then_inc(ln_centred, 1)

            def variance(m):
                pe.wait_ge(ln_squared, m + 1)
                for s in range(SUB):
                    last = pe.matmul(psN[0:SW, s:s + 1], sq[:, s * SW:(s + 1) * SW], mean_col[:, :],
                                     start=True, stop=True)
                last.then_inc(ln_var, 1)

            def broadcast(m):
                pe.wait_ge(ln_diag, m + 1)
                pe.matmul(psN[:, 0:BW], ones[0:SW, :], diag[:, :, :].rearrange("p s w -> p (s w)"),
                          start=True, stop=True).then_inc(ln_bcast, 1)

            def body(j, has2=True, has1=True, items=False):
                bank = psG[:, j % 2, 0:BW]
                for r in range(PIECES):
                    if items:
                        if r + AHEAD < QUADS:
                            item_quad(r + AHEAD)
                        pe.wait_ge(item_ready, (STARTS[r] + SIZES[r] - 1 + (r == LAST)) // 4 + 1)
                    for h in range(2):
                        s = 2 * r + h
                        pe.wait_ge(lo_ready, HALVES * j + s + 1)
                        for i in range(half_cols(r, h)[0] // BW):
                            c = STARTS[r] + h * HALF + i
                            rows = P if c < CH else TAIL
                            hi = a_hi[0:rows, s % CUT, i * BW:(i + 1) * BW]
                            lo = a_lo[0:rows, s % CUT, i * BW:(i + 1) * BW]
                            w_hi = item_hi[0:rows, c * HID:(c + 1) * HID]
                            w_lo = item_lo[0:rows, c * HID:(c + 1) * HID]
                            pe.matmul(bank, w_hi, hi, start=(c == 0), stop=False)
                            pe.matmul(bank, w_hi, lo, start=False, stop=False)
                            last = pe.matmul(bank, w_lo, hi, start=False, stop=(c == CH))
                        last.then_inc(halves_done, 1)
                    if items and r == 0:
                        broadcast(0)
                    if items and r == AT["wx"]:
                        pe.wait_ge(wx_in, 48)
                        pe.matmul(psW[:, :], centre[:, :], wx[:, :], start=True, stop=False)
                        pe.matmul(psW[:, :], inv_rows[:, :], bb, start=False, stop=True).then_inc(wx_psum, 1)
                    if items and r == AT["bias"]:
                        pe.wait_ge(w_in, 16 * 7)
                    if r == AT["bias"]:
                        pe.wait_ge(v_ready, j + 1)
                        pe.matmul(bank, wu[:, :], v[:, :], start=False, stop=False)
                    if has2 and r == AT["centre2"]:
                        pe.wait_ge(x1_ready, j)
                        centre_rows(j - 1, v_ready, j + 1)
                    if has2 and r == AT["var2"]:
                        variance(2 * j)
                    if has2 and r == AT["bcast2"]:
                        broadcast(2 * j)
                    if has1 and r == AT["centre1"]:
                        if has2:
                            pe.wait_ge(xb_in, 16 * j)
                        else:
                            pe.wait_ge(x_in[1], 16)
                        centre_rows(j + 1, ln_out if has2 else v_ready, j if has2 else 1)
                    if has1 and r == AT["var1"]:
                        variance(2 * j + 1)
                    if has1 and r == AT["bcast1"]:
                        broadcast(2 * j + 1)

            def item_quad(q):
                if q == 0:
                    pe.wait_ge(wi_in, 32)
                if q in PARTS:
                    pe.wait_ge(item_in[PARTS.index(q)], 16)
                if q >= 2:
                    pe.wait_ge(item_sum, q - 1)
                for c in range(4 * q, min(4 * q + 4, CH + 1)):
                    rows = P if c < CH else TAIL
                    last = pe.matmul(psI[0:rows, q % 2, (c % 4) * HID:(c % 4 + 1) * HID],
                                     u[:, W + c * P:W + c * P + rows], wi[:, :], start=True, stop=True)
                last.then_inc(item_psum, 1)

            pe.wait_ge(const_ready, 9)
            item_quad(0)
            item_quad(1)
            pe.wait_ge(x_in[0], 16)
            centre_rows(0, None, 0)
            item_quad(2)
            variance(0)
            body(0, has2=False, items=True)
            with nc.tensor.Fori(1, NB - 1) as j:
                body(j)
            body(NB - 1, has1=False)
            pe.wait_ge(x1_ready, NB)
            centre_rows(NB - 1, ln_out, NB - 1)
            variance(2 * NB - 1)
            broadcast(2 * NB - 1)

            def lstm(n, par, first_two=False, main=0):
                if not first_two:
                    pe.wait_ge(t_ready, 5 * n - 5)
                    pe.wait_ge(u_lo_ready, n - 1)
                else:
                    pe.wait_ge(first_lo_ready, n + 1)
                for q in GATES:
                    if main == 3 and q == GATES[-1]:
                        pe.wait_ge(gated, n - W - 1)
                    w_hi, w_lo = (w[:, q * HID:(q + 1) * HID] for w in (wx_hi, wx_lo))
                    bank = psZ[:, 4 * par + q, 0:XC]
                    pe.matmul(bank, w_hi, u_hi[:, par, :], start=True, stop=False)
                    pe.matmul(bank, w_hi, u_lo[:, par, :], start=False, stop=False)
                    pe.matmul(bank, w_lo, u_hi[:, par, :], start=False, stop=False)
                pe.wait_ge(h_ready, 2 * n + 1)
                for q in GATES:
                    pe.matmul(psZ[:, 4 * par + q, 0:K], wh[:, q * HID:(q + 1) * HID], H[:, par, :],
                              start=False, stop=True).then_inc(z_ready, 1)
                if main >= 2:
                    logits(par)

            def logits(par):
                pe.matmul(psZ[:, 4 * (1 - par) + GATES[-1], XC:XC + K], wd[:, :], H[:, par, :],
                          start=True, stop=True).then_inc(d_ready, 1)

            pe.wait_ge(prep, 14)
            pe.wait_ge(u_ready, NB)
            lstm(0, 0, first_two=True)
            lstm(1, 1, first_two=True)
            with nc.tensor.Fori(1, W // 2) as i:
                lstm(2 * i, 0)
                lstm(2 * i + 1, 1)
            pe.wait_ge(wd_ready, 1)
            lstm(W, 0, main=1)
            lstm(W + 1, 1, main=2)
            with nc.tensor.Fori(W // 2 + 1, STEPS // 2) as i:
                lstm(2 * i, 0, main=3)
                lstm(2 * i + 1, 1, main=3)
            pe.wait_ge(h_ready, 2 * STEPS + 1)
            pe.wait_ge(t_ready, 5 * STEPS)
            logits(0)
            pe.wait_ge(check, 5)
            pe.wait_ge(th_ready, 2 * STEPS)
            pe.matmul(psZ[:, 0, 0:1], ones[:, :], okmin[:, :], start=True, stop=True).then_inc(ok_sum, 1)

            pe.wait_ge(flag_ready, 1)
            redo = pe.value_load(flag[0:1, 0:1], min_val=0, max_val=1)
            with pe.If(redo > 0):
                with nc.tensor.Fori(0, N) as t:
                    pe.wait_ge(g_h, t + 1)
                    for q in range(4):
                        pe.matmul(psZ[:, 0, q:q + 1], wx[:, q * HID:(q + 1) * HID], u[:, ds(W + t, 1)],
                                  start=True, stop=False)
                        last = pe.matmul(psZ[:, 0, q:q + 1], wh[:, q * HID:(q + 1) * HID], H[:, 0, 0:1],
                                         start=False, stop=True)
                    last.then_inc(g_z, 1)
                pe.wait_ge(g_hist, N)
                with nc.tensor.Fori(0, NB) as f:
                    pe.wait_ge(g_out, 4 * f + 1)
                    pe.matmul(psZ[:, 2, 0:BW], wd[:, :], y[:, ds(f * BW, BW)], start=True, stop=True)\
                        .then_inc(g_d, 1)

        @block.vector
        def _(dve):
            def eps(m):
                dve.wait_ge(ln_var, m + 1)
                dve.tensor_scalar(var[:, :], psN[0:SW, 0:SUB], EPS, None, ALU.add).then_inc(ln_eps, 1)

            def diagonal(m):
                dve.wait_ge(ln_rstd, m + 1)
                dve.tensor_tensor(diag[:, :, :], ident[0:SW, 0:SW].unsqueeze(1).to_broadcast([SW, SUB, SW]),
                                  rstd[:, :].unsqueeze(2).to_broadcast([SW, SUB, SW]), ALU.mult)\
                    .then_inc(ln_diag, 1)

            def norm1(m):
                dve.wait_ge(ln_bcast, m + 1)
                dve.tensor_tensor(v[:, :], xc[:, :], psN[:, 0:BW], ALU.mult).then_inc(v_ready, 1)

            def norm2(m):
                dve.wait_ge(ln_bcast, m + 1)
                dve.tensor_tensor(un[:, :], xc[:, :], psN[:, 0:BW], ALU.mult).then_inc(ln_out, 1)

            def add_relu(j):
                dve.wait_ge(relu_done, j + 1)
                dve.tensor_tensor(xb[:, j % 2, :], xb[:, j % 2, :], rl[:, :], ALU.add).then_inc(x1_ready, 1)

            def split_lo(j, r, h):
                s = 2 * r + h
                n, at = half_cols(r, h)
                dve.wait_ge(hi_ready, HALVES * j + s + 1)
                dve.tensor_tensor(a_lo[:, s % CUT, 0:n], raw[:, r % RAW, at:at + n],
                                  a_hi[:, s % CUT, 0:n].bitcast(f32), ALU.subtract).then_inc(lo_ready, 1)

            def item_sum_part(q):
                n = min(4, CH + 1 - 4 * q)
                dve.wait_ge(item_psum, q + 1)
                if q < QUADS - 1:
                    dst = u[:, W + 4 * q * P:W + (4 * q + n) * P]
                    dve.tensor_tensor(dst.rearrange("p (c h) -> p c h", h=HID),
                                      psI[:, q % 2, 0:n * HID].rearrange("p (c h) -> p c h", h=HID),
                                      bi[:, :].unsqueeze(1).to_broadcast([P, n, HID]), ALU.add)\
                        .then_inc(item_sum, 1)
                    return
                dve.memset(sq[:, 0:n * HID], 0.0).then_inc(prep, 1)
                dve.wait_ge(prep, 1)
                for c0, c1, rows in ((0, n - 1, P), (n - 1, n, TAIL)):
                    dve.tensor_tensor(sq[0:rows, c0 * HID:c1 * HID].rearrange("p (c h) -> p c h", h=HID),
                                      psI[0:rows, q % 2, c0 * HID:c1 * HID].rearrange("p (c h) -> p c h", h=HID),
                                      bi[0:rows, :].unsqueeze(1).to_broadcast([rows, c1 - c0, HID]), ALU.add)\
                        .then_inc(item_sum if rows == TAIL else prep, 1)
                dve.wait_ge(prep, 2)

            def item_lo_part(q):
                n = min(4, CH + 1 - 4 * q)
                src = u[:, W + 4 * q * P:W + (4 * q + n) * P] if q < QUADS - 1 else sq[:, 0:n * HID]
                dve.wait_ge(item_hi_ready, q + 1)
                dve.tensor_tensor(item_lo[:, 4 * q * HID:(4 * q + n) * HID], src,
                                  item_hi[:, 4 * q * HID:(4 * q + n) * HID].bitcast(f32), ALU.subtract)\
                    .then_inc(item_ready, 1)

            def body(j, has2=True, has1=True, items=False):
                for r in range(PIECES):
                    split_lo(j, r, 0)
                    if items and r + 2 < QUADS:
                        item_sum_part(r + 2)
                    split_lo(j, r, 1)
                    if items and r + 1 < QUADS:
                        item_lo_part(r + 1)
                    if items and r == 0:
                        diagonal(0)
                    if items and r == 1:
                        norm1(0)
                    if has2 and r == AT["x1"]:
                        add_relu(j - 1)
                    if has2 and r == AT["eps2"]:
                        eps(2 * j)
                    if has2 and r == AT["diag2"]:
                        diagonal(2 * j)
                    if has2 and r == AT["norm2"]:
                        norm2(2 * j)
                    if has1 and r == AT["eps1"]:
                        eps(2 * j + 1)
                    if has1 and r == AT["diag1"]:
                        diagonal(2 * j + 1)
                    if has1 and r == AT["norm1"]:
                        norm1(2 * j + 1)

            dve.wait_ge(wi_in, 32)
            dve.wait_ge(const_ready, 9)
            item_sum_part(0)
            item_sum_part(1)
            item_lo_part(0)
            eps(0)
            body(0, has2=False, items=True)
            dve.wait_ge(wx_psum, 1)
            dve.tensor_scalar(wx[:, 0:2 * HID], psW[:, 0:2 * HID], 0.5, None, ALU.mult).then_inc(prep, 1)
            dve.tensor_scalar(wx[:, 2 * HID:3 * HID], psW[:, 2 * HID:3 * HID], 1.0, None, ALU.mult).then_inc(prep, 1)
            dve.tensor_scalar(wx[:, 3 * HID:4 * HID], psW[:, 3 * HID:4 * HID], 0.5, None, ALU.mult).then_inc(prep, 1)
            dve.wait_ge(w_in, 16 * 7)
            dve.tensor_scalar(wh[:, 0:2 * HID], wh[:, 0:2 * HID], 0.25, None, ALU.mult).then_inc(prep, 1)
            dve.tensor_scalar(wh[:, 2 * HID:3 * HID], wh[:, 2 * HID:3 * HID], 0.5, None, ALU.mult).then_inc(prep, 1)
            dve.tensor_scalar(wh[:, 3 * HID:4 * HID], wh[:, 3 * HID:4 * HID], 0.25, None, ALU.mult).then_inc(prep, 1)
            dve.tensor_tensor(wdc[:, :], wl[:, 1:2], wl[:, 0:1], ALU.subtract).then_inc(prep, 1)
            dve.tensor_tensor(thr0[:, :], bl[:, 0:1], bl[:, 1:2], ALU.subtract).then_inc(prep, 1)
            dve.tensor_scalar(hfw[:, :], fwc[:, :], 0.5, None, ALU.mult).then_inc(prep, 1)
            dve.tensor_scalar(mbw[:, :], bwc[:, :], -0.5, None, ALU.mult).then_inc(prep, 1)
            dve.wait_ge(prep, 12)
            dve.tensor_scalar(wx_hi[:, :], wx[:, :], 1.0, None, ALU.mult).then_inc(prep, 1)
            dve.wait_ge(prep, 13)
            dve.tensor_tensor(wx_lo[:, :], wx[:, :], wx_hi[:, :].bitcast(f32), ALU.subtract).then_inc(prep, 1)
            with nc.vector.Fori(1, NB - 1) as j:
                body(j)
            body(NB - 1, has1=False)
            add_relu(NB - 1)
            eps(2 * NB - 1)
            diagonal(2 * NB - 1)
            norm2(2 * NB - 1)

            dve.wait_ge(u_ready, NB)
            dve.memset(C[:, :], 0.0).then_inc(zeroed, 1)
            dve.memset(H[:, 0, :], 0.0).then_inc(h_ready, 1)
            dve.wait_ge(prep, 12)
            dve.tensor_tensor(dfb[:, :], hfw[:, :], mbw[:, :], ALU.add).then_inc(dfb_ready, 1)
            dve.tensor_scalar(thr[:, :], thr0[:, :], 2.0, None, ALU.mult).then_inc(wd_ready, 1)
            dve.tensor_scalar(wd[:, :], ones[:, :], wdc[:, 0:1], None, ALU.mult).then_inc(wd_ready, 1)
            dve.wait_ge(zeroed, 1)
            dve.wait_ge(h_ready, 1)

            dve.tensor_scalar(u_lo[:, :, K:XC], u[:, 0:XC - K].unsqueeze(1).to_broadcast([P, 2, XC - K]), 1.0, None,
                              ALU.mult)
            for m in range(2):
                dve.wait_ge(u_hi_ready, m + 1)
                dve.tensor_tensor(u_lo[:, m, 0:K], u[:, ds(m, K, L)], u_hi[:, m, 0:K].bitcast(f32), ALU.subtract)\
                    .then_inc(first_lo_ready, 1)

            def gate(s, par, first=False):
                dve.wait_ge(d_ready, s + 1)
                if not first:
                    dve.wait_ge(run_ready, s)
                    dve.wait_ge(own_ready, s)
                dve.scalar_tensor_tensor(gh[:, par, :], psZ[:, 4 * par + GATES[-1], XC:XC + K], thr[:, 0:1],
                                         H[:, 1 - par, :], ALU.is_gt, ALU.mult).then_inc(gated, 1)

            def own_term(s, par, first=False):
                dve.wait_ge(gated, s + 1)
                if not first:
                    dve.wait_ge(both_ready, s)
                dve.scalar_tensor_tensor(own[:, :], gh[:, par, :], mbw[:, 0:1], H[:, 1 - par, :],
                                         ALU.mult, ALU.add).then_inc(own_ready, 1)

            def lstm(n, par, boundary=False, last_row=None, first=False):
                halves = ((0, KH), (KH, K))
                dve.wait_ge(t_ready, 5 * n + 1)
                dve.scalar_tensor_tensor(fc[:, :], gt[:, 1, :], 1.0, C[:, :], ALU.add, ALU.mult)\
                    .then_inc(parts, 1)
                for x, (a, b) in enumerate(halves):
                    dve.wait_ge(t_ready, 5 * n + 3 + x)
                    dve.scalar_tensor_tensor(ig[:, a:b], gt[:, 0, a:b], 1.0, gt[:, 2, a:b], ALU.add, ALU.mult)\
                        .then_inc(parts, 1)
                for x, (a, b) in enumerate(halves):
                    dve.wait_ge(parts, 3 * n + 2 + x)
                    dve.scalar_tensor_tensor(C[:, a:b], fc[:, a:b], 0.5, ig[:, a:b], ALU.mult, ALU.add)\
                        .then_inc(c_ready, 1)
                if last_row is not None:
                    gate(last_row, 1 - par, first)
                dve.wait_ge(t_ready, 5 * n + 5)
                for x, (a, b) in enumerate(halves):
                    dve.wait_ge(th_ready, 2 * n + 1 + x)
                    dve.scalar_tensor_tensor(H[:, 1 - par, a:b], gt[:, 3, a:b], 1.0, th[:, a:b], ALU.add, ALU.mult)\
                        .then_inc(bound if boundary else h_ready, 1)
                if boundary:
                    dve.wait_ge(bound, 2)
                    dve.memset(C[:, 0:1], 0.0).then_inc(zeroed, 1)
                    dve.memset(H[:, 0, 0:1], 0.0).then_inc(h_ready, 2)
                    dve.wait_ge(zeroed, 2)
                    dve.wait_ge(h_ready, 2 * n + 3)
                    dve.tensor_copy(C0[:, :], C[:, :]).then_inc(zeroed, 1)
                    dve.tensor_copy(H0[:, :], H[:, 0, :]).then_inc(zeroed, 1)
                if last_row is not None:
                    own_term(last_row, 1 - par, first)

            with nc.vector.Fori(0, W // 2 - 1) as i:
                lstm(2 * i, 0)
                lstm(2 * i + 1, 1)
            lstm(W - 2, 0)
            lstm(W - 1, 1, boundary=True)
            dve.wait_ge(wd_ready, 2)
            lstm(W, 0)
            lstm(W + 1, 1, last_row=0, first=True)
            with nc.vector.Fori(1, L // 2) as i:
                lstm(W + 2 * i, 0, last_row=2 * i - 1)
                lstm(W + 2 * i + 1, 1, last_row=2 * i)
            dve.wait_ge(h_ready, 2 * STEPS + 1)
            gate(L - 1, 1)
            own_term(L - 1, 1)

            dve.wait_ge(c_ready, 2 * STEPS)
            dve.wait_ge(zeroed, 4)
            dve.tensor_tensor(dif[:, 0:K - 1], H[:, 0, 0:K - 1], H0[:, 1:K], ALU.subtract).then_inc(check, 1)
            dve.tensor_tensor(dif[:, K - 1:], C[:, 0:K - 1], C0[:, 1:K], ALU.subtract).then_inc(check, 1)
            dve.wait_ge(check, 2)
            dve.tensor_tensor(dif[:, :], dif[:, :], dif[:, :], ALU.mult).then_inc(check, 1)
            dve.wait_ge(check, 3)
            dve.tensor_scalar(dif[:, :], dif[:, :], HANDOVER_TOL ** 2, None, ALU.is_le).then_inc(check, 1)
            dve.wait_ge(check, 4)
            dve.tensor_reduce(okmin[:, :], dif[:, :], mybir.AxisListType.X, ALU.min).then_inc(check, 1)
            dve.memset(cum[:, 0:1], 0.0).then_inc(cum_ready, 1)
            dve.wait_ge(run_ready, L + 1)
            dve.wait_ge(cum_ready, 1)
            dve.tensor_tensor_scan(cum[:, 1:K + 1], run[:, 0, :], run[:, 0, :], cum[:, 0:1], ALU.add, ALU.bypass)\
                .then_inc(cum_ready, 1)
            dve.wait_ge(cum_ready, 2)
            dve.wait_ge(ok_sum, 1)
            dve.tensor_scalar(flag[:, :], psZ[:, 0, 0:1], float(P) - 0.5, None, ALU.is_lt).then_inc(flag_ready, 1)
            dve.wait_ge(flag_ready, 1)
            redo = dve.value_load(flag[0:1, 0:1], min_val=0, max_val=1)
            with dve.If(redo > 0):
                dve.wait_ge(y_ready, L)
                dve.memset(C[:, 0:1], 0.0).then_inc(zeroed, 1)
                dve.wait_ge(zeroed, 5)
                dve.memset(H[:, 0, 0:1], 0.0).then_inc(g_h, 1)
                with nc.vector.Fori(0, N) as t:
                    dve.wait_ge(g_t, t + 1)
                    dve.scalar_tensor_tensor(fc[:, 0:1], gt[:, 0, 1:2], 1.0, C[:, 0:1], ALU.add, ALU.mult)\
                        .then_inc(g_parts, 1)
                    dve.scalar_tensor_tensor(ig[:, 0:1], gt[:, 0, 0:1], 1.0, gt[:, 0, 2:3], ALU.add, ALU.mult)\
                        .then_inc(g_parts, 1)
                    dve.wait_ge(g_parts, 2 * t + 2)
                    dve.scalar_tensor_tensor(C[:, 0:1], fc[:, 0:1], 0.5, ig[:, 0:1], ALU.mult, ALU.add)\
                        .then_inc(g_c, 1)
                    dve.wait_ge(g_th, t + 1)
                    dve.scalar_tensor_tensor(H[:, 0, 0:1], gt[:, 0, 3:4], 1.0, th[:, 0:1], ALU.add, ALU.mult)\
                        .then_inc(g_h, 1)
                    dve.wait_ge(g_h, t + 2)
                    dve.tensor_copy(y[:, ds(t, 1)], H[:, 0, 0:1]).then_inc(g_hist, 1)
                dve.wait_ge(g_hist, N)
                dve.memset(g_cum[:, BW:BW + 1], 0.0).then_inc(g_out, 1)
                with nc.vector.Fori(0, NB) as f:
                    rows = y[:, ds(f * BW, BW)]
                    dve.wait_ge(g_out, 4 * f + 1)
                    dve.tensor_copy(g_cum[:, 0:1], g_cum[:, BW:BW + 1]).then_inc(g_out, 1)
                    dve.wait_ge(g_d, f + 1)
                    dve.scalar_tensor_tensor(g_gh[:, :], psZ[:, 2, 0:BW], thr[:, 0:1], rows, ALU.is_gt, ALU.mult)\
                        .then_inc(g_out, 1)
                    dve.wait_ge(g_out, 4 * f + 3)
                    dve.tensor_tensor_scan(g_cum[:, 1:BW + 1], g_gh[:, :], g_gh[:, :], g_cum[:, 0:1],
                                           ALU.add, ALU.bypass).then_inc(g_out, 1)
                    dve.scalar_tensor_tensor(rows, g_gh[:, :], mbw[:, 0:1], rows, ALU.mult, ALU.add)\
                        .then_inc(g_terms, 1)
                    dve.wait_ge(g_out, 4 * f + 4)
                    dve.wait_ge(g_terms, 2 * f + 1)
                    dve.scalar_tensor_tensor(rows, g_cum[:, 0:BW], dfb[:, 0:1], rows, ALU.mult, ALU.add)\
                        .then_inc(g_terms, 1)
                    dve.wait_ge(g_terms, 2 * f + 2)
                    dve.tensor_tensor(rows, rows, x1[:, ds(f * BW, BW)], ALU.add).then_inc(g_out, 1)
                dve.wait_ge(g_out, 4 * NB + 1)
                dve.memset(cum[:, 0:K], 0.0).then_inc(g_end, 1)
                dve.tensor_copy(cum[:, K:K + 1], g_cum[:, BW:BW + 1]).then_inc(g_end, 1)
                dve.wait_ge(g_end, 2)
            dve.scalar_tensor_tensor(total[:, :], cum[:, K:K + 1], -1.0, mbw[:, :], ALU.mult, ALU.mult)\
                .then_inc(total_ready, 1)
            dve.wait_ge(total_ready, 1)
            dve.tensor_scalar(shift[:, :], cum[:, 0:K], dfb[:, 0:1], total[:, 0:1], ALU.mult, ALU.add)\
                .then_inc(shift_ready, 1)
            dve.wait_ge(shift_ready, 1)
            dve.wait_ge(y_ready, L)
            for f in range(OUTS):
                if not by_pool(f):
                    dve.tensor_tensor(chunks_of(y, f), chunks_of(y, f), shift_of(f), ALU.add)\
                        .then_inc(out_ready_v, 1)


def kernel(x, adj, L0_gnn_item_feat, L0_gnn_W_item, L0_gnn_b_item, L0_gnn_W_user, L0_gnn_b_user,
           L0_ffn_W_ih, L0_ffn_W_hh, L0_ffn_b_ih, L0_ffn_b_hh, L0_ffn_W_lin, L0_ffn_b_lin,
           L0_ffn_fw_att, L0_ffn_bw_att):
    import numpy as np
    import concourse.bacc as bacc
    from concourse.bass_utils import run_bass_kernel_spmd

    adjT = np.asarray(adj).T
    main = adjT[:CH * P].reshape(CH, P, NB, BW).transpose(2, 1, 0, 3).reshape(NB, P, CH * BW)
    short = adjT[CH * P:].reshape(TAIL, NB, BW).transpose(1, 0, 2)
    host = [
        ("xT", np.asarray(x).T), ("itemT", np.asarray(L0_gnn_item_feat).T),
        ("adj_main", main), ("adj_tail", short),
        ("w_itemT", np.asarray(L0_gnn_W_item).T), ("b_item", np.asarray(L0_gnn_b_item).reshape(1, HID)),
        ("w_userT", np.asarray(L0_gnn_W_user).T), ("b_user", np.asarray(L0_gnn_b_user).reshape(HID, 1)),
        ("w_ihT", np.asarray(L0_ffn_W_ih).T), ("w_hhT", np.asarray(L0_ffn_W_hh).T),
        ("b_ih", np.asarray(L0_ffn_b_ih).reshape(1, 4 * HID)), ("b_hh", np.asarray(L0_ffn_b_hh).reshape(1, 4 * HID)),
        ("w_linT", np.asarray(L0_ffn_W_lin).T), ("b_lin", np.asarray(L0_ffn_b_lin).reshape(1, 2)),
        ("fw", np.asarray(L0_ffn_fw_att).reshape(HID, 1)), ("bw", np.asarray(L0_ffn_bw_att).reshape(HID, 1)),
    ]
    nc = bacc.Bacc("TRN2", target_bir_lowering=False, num_devices=1)
    arrays, args = {}, []
    for name, a in host:
        a = np.ascontiguousarray(a)
        arrays[f"in_{name}"] = a
        args.append(nc.dram_tensor(f"in_{name}", a.shape, mybir.dt.from_np(a.dtype), kind="ExternalInput").ap())
    out = nc.dram_tensor("out_0", (HID, N), mybir.dt.float32, kind="ExternalOutput").ap()
    program(nc, *args, out)
    r = run_bass_kernel_spmd(nc, [arrays], core_ids=[0])
    return np.ascontiguousarray(r.results[0]["out_0"].T)
```
